# Optimizing a Trainium2 kernel written in Bass

```python
import numpy as np
import jax
import jax.numpy as jnp

def _softmax(x, axis=-1):
    return jax.nn.softmax(x, axis=axis)

def _gelu(x):
    return jax.nn.gelu(x, approximate=True)

def _silu(x):
    return jax.nn.silu(x)

def _sigmoid(x):
    return jax.nn.sigmoid(x)

def _layernorm(x, axis=-1, eps=1e-05):
    m = jnp.mean(x, axis=axis, keepdims=True)
    v = jnp.var(x, axis=axis, keepdims=True)
    return (x - m) / jnp.sqrt(v + eps)

def _scatter_add(tgt, idx, src, axis=0):
    return tgt.at[idx].add(src)

def _segment_sum(src, seg, n):
    return jax.ops.segment_sum(src, seg, n)
kernel_name = 'mk_macaron_d1_jaxref_r4_000b4e'

def setup_inputs(seed: int=0):
    np.random.seed(seed)
    _w = jnp.asarray

    def _L0_attn_setup():
        import jax, jax.numpy as jnp
        import numpy as np
        B, S, HIDDEN, H = (4, 1024, 512, 16)
        HD = HIDDEN // H

        def apply_rope(x, inv_freq):
            seq_len = x.shape[1]
            t = jnp.arange(seq_len, dtype=jnp.float32)[:, None]
            angle = t * inv_freq[None, :]
            sin = jnp.sin(angle)[None, :, None, :]
            cos = jnp.cos(angle)[None, :, None, :]
            x1, x2 = (x[..., ::2], x[..., 1::2])
            return jnp.concatenate([x1 * cos - x2 * sin, x1 * sin + x2 * cos], axis=-1)
        key = jax.random.key(seed)
        ks = jax.random.split(key, 5)
        x = jax.random.normal(ks[0], (B, S, HIDDEN), dtype=jnp.float32)
        scale = 1.0 / np.sqrt(HIDDEN)
        wq = jax.random.normal(ks[1], (HIDDEN, HIDDEN), dtype=jnp.float32) * scale
        wk = jax.random.normal(ks[2], (HIDDEN, HIDDEN), dtype=jnp.float32) * scale
        wv = jax.random.normal(ks[3], (HIDDEN, HIDDEN), dtype=jnp.float32) * scale
        wo = jax.random.normal(ks[4], (HIDDEN, HIDDEN), dtype=jnp.float32) * scale
        inv_freq = (1.0 / 10000.0 ** (np.arange(0, HD, 2, dtype=np.float32) / HD)).astype(np.float32)
        inv_freq = jnp.asarray(inv_freq)
        return {'x': x, 'wq': wq, 'wk': wk, 'wv': wv, 'wo': wo, 'inv_freq': inv_freq}
    _L0_attn_in = _L0_attn_setup()

    def _L0_ffn_setup():
        import jax, jax.numpy as jnp
        import numpy as np
        B, S, D, H = (4, 512, 512, 2048)

        def fwht(x):
            orig_shape = x.shape
            n = orig_shape[-1]
            x = x.reshape(-1, n)
            h = 1
            while h < n:
                xb = x.reshape(-1, n // (2 * h), 2, h)
                a = xb[:, :, 0, :]
                b = xb[:, :, 1, :]
                x = jnp.stack([a + b, a - b], axis=2).reshape(-1, n)
                h *= 2
            scale = jnp.asarray(1.0 / np.sqrt(n), dtype=x.dtype)
            return (x * scale).reshape(orig_shape)
        key = jax.random.key(seed)
        kx, k1, k2, k3 = jax.random.split(key, 4)
        x = jax.random.normal(kx, (B, S, D), dtype=jnp.float32)
        W1 = jax.random.normal(k1, (H, D), dtype=jnp.float32) * (1.0 / np.sqrt(D))
        W2 = jax.random.normal(k2, (D, H), dtype=jnp.float32) * (1.0 / np.sqrt(H))
        W3 = jax.random.normal(k3, (H, D), dtype=jnp.float32) * (1.0 / np.sqrt(D))
        return {'x': x, 'W1': W1, 'W2': W2, 'W3': W3}
    _L0_ffn_in = _L0_ffn_setup()
    _d = {'L0_attn_x': _L0_attn_in['x'], 'L0_attn_wq': _L0_attn_in['wq'], 'L0_attn_wk': _L0_attn_in['wk'], 'L0_attn_wv': _L0_attn_in['wv'], 'L0_attn_wo': _L0_attn_in['wo'], 'L0_attn_inv_freq': _L0_attn_in['inv_freq'], 'L0_ffn_W1': _L0_ffn_in['W1'], 'L0_ffn_W2': _L0_ffn_in['W2'], 'L0_ffn_W3': _L0_ffn_in['W3']}
    _x0 = _d['L0_attn_x']
    _d['L0_attn_x'] = jax.random.normal(jax.random.fold_in(jax.random.key(seed), 1), (4, 1024, 512), dtype=_x0.dtype)
    del _x0
    return _d

def reference(L0_attn_x, L0_attn_wq, L0_attn_wk, L0_attn_wv, L0_attn_wo, L0_attn_inv_freq, L0_ffn_W1, L0_ffn_W2, L0_ffn_W3):

    def _L0_attn_ref(x, wq, wk, wv, wo, inv_freq):
        import jax, jax.numpy as jnp
        import numpy as np
        B, S, HIDDEN, H = (4, 1024, 512, 16)
        HD = HIDDEN // H

        def apply_rope(x, inv_freq):
            seq_len = x.shape[1]
            t = jnp.arange(seq_len, dtype=jnp.float32)[:, None]
            angle = t * inv_freq[None, :]
            sin = jnp.sin(angle)[None, :, None, :]
            cos = jnp.cos(angle)[None, :, None, :]
            x1, x2 = (x[..., ::2], x[..., 1::2])
            return jnp.concatenate([x1 * cos - x2 * sin, x1 * sin + x2 * cos], axis=-1)
        b, s, _ = x.shape
        q = (x @ wq.T).reshape(b, s, H, HD)
        k = (x @ wk.T).reshape(b, s, H, HD)
        v = (x @ wv.T).reshape(b, s, H, HD)
        q = apply_rope(q, inv_freq)
        k = apply_rope(k, inv_freq)
        scores = jnp.einsum('bshd,bstd->bsht', q, k) / jnp.sqrt(jnp.float32(HD))
        weights = jax.nn.softmax(scores, axis=-1)
        attn = jnp.einsum('bsht,bstd->bshd', weights, v)
        attn = attn.reshape(b, s, HIDDEN)
        return attn @ wo.T

    def _L0_ffn_ref(x, W1, W2, W3):
        import jax, jax.numpy as jnp
        import numpy as np
        B, S, D, H = (4, 512, 512, 2048)

        def fwht(x):
            orig_shape = x.shape
            n = orig_shape[-1]
            x = x.reshape(-1, n)
            h = 1
            while h < n:
                xb = x.reshape(-1, n // (2 * h), 2, h)
                a = xb[:, :, 0, :]
                b = xb[:, :, 1, :]
                x = jnp.stack([a + b, a - b], axis=2).reshape(-1, n)
                h *= 2
            scale = jnp.asarray(1.0 / np.sqrt(n), dtype=x.dtype)
            return (x * scale).reshape(orig_shape)
        up_gate = jnp.einsum('bsd,hd->bsh', x, W1)
        up_lin = jnp.einsum('bsd,hd->bsh', x, W3)
        hidden = jax.nn.silu(up_gate) * up_lin
        hidden = fwht(hidden)
        out = jnp.einsum('bsh,dh->bsd', hidden, W2)
        return out
    x = L0_attn_x
    x = x + 0.5 * _L0_ffn_ref(_layernorm(x, axis=-1), L0_ffn_W1, L0_ffn_W2, L0_ffn_W3)
    x = x + _L0_attn_ref(_layernorm(x, axis=-1), L0_attn_wq, L0_attn_wk, L0_attn_wv, L0_attn_wo, L0_attn_inv_freq)
    x = x + 0.5 * _L0_ffn_ref(_layernorm(x, axis=-1), L0_ffn_W1, L0_ffn_W2, L0_ffn_W3)
    return x

_drawn_inputs = setup_inputs


def setup_inputs(seed=0):
    import zlib

    import numpy as np

    out = dict(_drawn_inputs(seed))
    spreads = {}
    factors = {}
    for name, (base, spread) in spreads.items():
        noise = np.random.default_rng([zlib.crc32(name.encode()), seed]).standard_normal(out[name].shape)
        drawn = base * np.exp(spread * noise) if base else spread * noise
        out[name] = jnp.asarray(drawn.astype(out[name].dtype))
    for name, factor in factors.items():
        out[name] = (out[name] * factor).astype(out[name].dtype)
    return out
```

```python
from contextlib import ExitStack

import numpy as np
import concourse.bass as bass
from concourse import mybir

FP32 = mybir.dt.float32
FP32R = mybir.dt.float32r
ALU = mybir.AluOpType
ACT = mybir.ActivationFunctionType
AX = mybir.AxisListType

B, S, D, HID = 4, 1024, 512, 2048
HEADS = 16
HD = D // HEADS
NF = HD // 2
P = 128
TOK = 512
TILES = B * S // TOK
SUBS = TOK // P
KT = D // P
HT = HID // P
POS = S // P
EPS = 1e-5
DOWN_SCALE = 0.5 / float(np.sqrt(HID))
SCORE_SCALE = 1.0 / float(np.sqrt(HD))
Q, K, V, O = range(4)
ADDS_TILE = 4


class Count:

    def __init__(self, sem):
        self.sem, self.start, self.k = sem, 0, 0

    def mark(self, ins):
        ins.then_inc(self.sem, 1)
        self.k += 1
        return self.start + self.k


def wide(ap, dim, n):
    shape = list(ap.shape)
    shape[dim] = n
    return ap.broadcast_to(shape)


def build(nc, x, up_raw, w2t, attn_raw, inv_freq, hadamard, identity, out):
    ctx = ExitStack()
    with ctx:
        def sb(name, shape, dt=FP32):
            return ctx.enter_context(nc.sbuf_tensor(name, shape, dt))

        def sem(name):
            return ctx.enter_context(nc.semaphore(name))

        up_pairs = nc.dram_tensor("up_pairs", [HT, P, 2 * 2 * KT * P], FP32).ap()
        down_pairs = nc.dram_tensor("down_pairs", [HT, P, 2 * D], FP32).ap()

        w_attn = sb("w_attn", [P, 4, 2, KT, D], FP32R)
        w_up = sb("w_up", [P, 2, 2, 2, KT, P], FP32R)
        w_down = sb("w_down", [P, 2, 2, D], FP32R)
        xt = [sb(f"xt{i}", [P, 2, KT, TOK], FP32R) for i in range(2)]
        hid = sb("hid", [P, 2, 2, TOK], FP32R)
        gated = sb("gated", [P, 2, TOK])
        x_in = sb("x_in", [P, SUBS, D])
        x_mid = sb("x_mid", [P, SUBS, D])
        x_out = sb("x_out", [P, SUBS, D])
        tok = sb("tok", [P, 4 * SUBS, D])
        prod = sb("prod", [P, 2, 2 * HEADS * HD])
        scores = sb("scores", [P, HEADS, HEADS])
        head_max = sb("head_max", [P, HEADS])
        head_sum = sb("head_sum", [P, HEADS])
        cos_t = sb("cos_t", [P, TILES * SUBS, NF])
        sin_t = sb("sin_t", [P, TILES * SUBS, NF])
        ident = sb("ident", [P, P])
        hada = sb("hada", [P, P])
        freq = sb("freq", [P, NF])
        stats = sb("stats", [P, SUBS, 6])
        mean_var = sb("mean_var", [P, SUBS, 2])
        rstd = sb("rstd", [P, SUBS])
        eps = sb("eps", [P, SUBS])
        mixed = sb("mixed", [P, HEADS, HD])
        carrier = sb("carrier", [P, 64])
        minus_half = sb("minus_half", [P, SUBS])

        acc = ctx.enter_context(nc.psum_tensor("acc", [P, SUBS, TOK], FP32))
        gu = ctx.enter_context(nc.psum_tensor("gu", [P, 4, TOK], FP32))

        s_const = sem("s_const")
        s_w2 = sem("s_w2")
        s_x = sem("s_x")
        s_attn_raw = [sem(f"s_attn_raw{m}") for m in range(4)]
        s_up_raw = [sem(f"s_up_raw{i}") for i in range(2)]
        s_up_loaded = [sem(f"s_up_loaded{i}") for i in range(2)]
        s_down_loaded = [sem(f"s_down_loaded{i}") for i in range(2)]
        s_up_stored = [sem(f"s_up_stored{i}") for i in range(2)]
        s_down_stored = [sem(f"s_down_stored{i}") for i in range(2)]
        s_freq_out = sem("s_freq_out")
        s_tabs = sem("s_tabs")
        s_trig = sem("s_trig")
        s_angle = sem("s_angle")
        s_fwht = sem("s_fwht")
        s_had_ps = sem("s_had_ps")
        s_down_hi = sem("s_down_hi")
        s_down_lo = sem("s_down_lo")
        s_up_hi = sem("s_up_hi")
        s_up_lo = sem("s_up_lo")
        s_wattn = sem("s_wattn")
        s_up_done = sem("s_up_done")
        s_silu = sem("s_silu")
        s_h = sem("s_h")
        s_hid_hi = sem("s_hid_hi")
        s_hid_lo = sem("s_hid_lo")
        s_down_done = sem("s_down_done")
        s_added = sem("s_added")
        s_var = sem("s_var")
        s_eps = sem("s_eps")
        s_rstd = sem("s_rstd")
        s_ln = sem("s_ln")
        s_xt_ps = sem("s_xt_ps")
        s_xt_hi = sem("s_xt_hi")
        s_xt_lo = sem("s_xt_lo")
        s_wo = sem("s_wo")
        s_x2 = sem("s_x2")
        s_mid = sem("s_mid")
        s_qk = sem("s_qk")
        s_rope = sem("s_rope")
        s_v_ps = sem("s_v_ps")
        s_v = sem("s_v")
        s_shift = sem("s_shift")
        s_exp = sem("s_exp")
        s_attn = sem("s_attn")
        s_dve = sem("s_dve")
        s_pool = sem("s_pool")

        block = ctx.enter_context(nc.Block())

        LAST = TILES - 1

        x_v = x.rearrange("(i s p) d -> i p s d", p=P, s=SUBS)
        out_v = out.rearrange("(i s p) d -> i p s d", p=P, s=SUBS)

        @block.sync
        def _(sp):
            def up_slot(u):
                return w_up[:, u].rearrange("p a b c d -> p (a b c d)").bitcast(FP32)

            def down_slot(u):
                return w_down[:, u].rearrange("p a n -> p (a n)").bitcast(FP32)

            def slab(pairs, j):
                return pairs[bass.ds(j, 1)].rearrange("o p n -> p (o n)")

            sp.dma_start(tok[:], w2t.rearrange("a p n -> p a n")).then_inc(s_w2, 16)
            sp.dma_start(hada[:], hadamard).then_inc(s_const, 16)
            sp.dma_start(ident[:], identity).then_inc(s_const, 16)
            sp.dma_start(freq[:], wide(inv_freq.rearrange("(a f) -> a f", a=1), 0, P)).then_inc(s_freq_out, 16)
            sp.dma_start(x_in[:], x_v[0]).then_inc(s_x, 16)
            for j in range(2):
                sp.dma_start(prod[:, j, :], up_raw[j]).then_inc(s_up_raw[j], 16)
            for a in range(HT):
                sp.wait_ge(s_down_hi, a + 1)
                sp.wait_ge(s_down_lo, a + 1)
                sp.dma_start(down_pairs[a], down_slot(a % 2)).then_inc(s_down_stored[a % 2], 16)
            for u in range(2):
                sp.wait_ge(s_down_stored[u], 8 * HT)
            for m in range(4):
                sp.dma_start(tok[:, 4 * m:4 * m + 4, :], attn_raw[m]).then_inc(s_attn_raw[m], 16)
            for j in range(2):
                sp.dma_start(down_slot(j), down_pairs[j]).then_inc(s_down_loaded[j], 16)

            with sp.Fori(0, HT // 2 - 1) as jj:
                for u in range(2):
                    sp.wait_ge(s_up_hi, 2 * jj + u + 1)
                    sp.wait_ge(s_up_lo, 2 * jj + u + 1)
                    sp.dma_start(slab(up_pairs, 2 * jj + u), up_slot(u)).then_inc(s_up_stored[u], 16)
                    sp.dma_start(prod[:, u, :],
                                 slab(up_raw, 2 * jj + u + 2)).then_inc(s_up_raw[u], 16)
                    sp.wait_ge(s_down_done, 2 * jj + u + 1)
                    sp.dma_start(down_slot(u), slab(down_pairs, 2 * jj + u + 2)).then_inc(s_down_loaded[u], 16)
            for u in range(2):
                j = HT - 2 + u
                sp.wait_ge(s_up_hi, j + 1)
                sp.wait_ge(s_up_lo, j + 1)
                sp.dma_start(up_pairs[j], up_slot(u)).then_inc(s_up_stored[u], 16)
            for u in range(2):
                sp.wait_ge(s_up_stored[u], 8 * HT)

            def load_up(j, u):
                sp.dma_start(up_slot(u), slab(up_pairs, j)).then_inc(s_up_loaded[u], 16)

            def load_down(j, u):
                sp.dma_start(down_slot(u), slab(down_pairs, j)).then_inc(s_down_loaded[u], 16)

            def weights(b):
                with sp.Fori(0, HT // 2) as jj:
                    for u in range(2):
                        sp.wait_ge(s_up_done, HT * b + 2 * jj + u - 1)
                        load_up(2 * jj + u, u)
                        sp.wait_ge(s_down_done, HT * b + 2 * jj + u - 1)
                        load_down(2 * jj + u, u)

            sp.wait_ge(s_mid, 1)
            sp.dma_start(x_in[:], x_v[1]).then_inc(s_x, 16)

            def iteration(i, last):
                weights(2 * i - 1)
                if not last:
                    sp.wait_ge(s_mid, i + 1)
                    sp.dma_start(x_in[:].rearrange("p s d -> p s d"),
                                 x_v[bass.ds(i + 1, 1)].rearrange("o p s d -> p (o s) d")).then_inc(s_x, 16)
                weights(2 * i)
                sp.wait_ge(s_added, SUBS * (2 * i + 1))
                sp.dma_start(out_v[bass.ds(i - 1, 1)].rearrange("o p s d -> p (o s) d"), x_out[:]).then_inc(s_freq_out, 16)

            with sp.Fori(1, LAST) as i:
                iteration(i, False)
            iteration(LAST, True)
            weights(2 * TILES - 1)
            sp.wait_ge(s_added, SUBS * 2 * TILES)
            sp.dma_start(out_v[LAST], x_out[:]).then_inc(s_freq_out, 16)
            sp.wait_ge(s_freq_out, 16 * (TILES + 1))

        @block.tensor
        def _(pe):
            def products(o, w_hi, w_lo, m_hi, m_lo, first, last):
                nc.tensor.matmul(o, w_hi, m_hi, start=first, stop=False)
                nc.tensor.matmul(o, w_hi, m_lo, start=False, stop=False)
                return nc.tensor.matmul(o, w_lo, m_hi, start=False, stop=last)

            def up(n, u, X):
                for w in range(2):
                    for k in range(KT):
                        ins = products(gu[:, 2 * u + w, :], w_up[:, u, 0, w, k, :], w_up[:, u, 1, w, k, :],
                                       X[:, 0, k, :], X[:, 1, k, :], k == 0, k == KT - 1)
                ins.then_inc(s_up_done, 1)

            def down(n, u, first, last):
                pe.wait_ge(s_hid_lo, n + 1)
                for s in range(SUBS):
                    ins = products(acc[:, s, :], hid[:, u, 0, s * P:(s + 1) * P], hid[:, u, 1, s * P:(s + 1) * P],
                                   w_down[:, u, 0, :], w_down[:, u, 1, :], first, last)
                ins.then_inc(s_down_done, 1)

            def transposes(src, bank, ks):
                for k in ks:
                    for s in range(SUBS):
                        ins = nc.tensor.transpose(bank[:, k, s * P:(s + 1) * P], tok[:, src(s), k * P:(k + 1) * P], ident[:])
                    ins.then_inc(s_xt_ps, 1)

            def ffn(b, X, build, before_build=None, src=None, first_block=False):
                n0 = HT * b

                def slabs(j, jj, u, kind):
                    if kind == "up":
                        if first_block:
                            pe.wait_ge(s_up_hi, j + 1)
                            pe.wait_ge(s_up_lo, j + 1)
                        else:
                            pe.wait_ge(s_up_loaded[u], 16 * (HT // 2 * (b - 1) + jj + 1))
                    else:
                        pe.wait_ge(s_down_loaded[u], 16 * (HT // 2 * b + jj + 1))

                slabs(0, 0, 0, "up")
                up(n0, 0, X)
                slabs(1, 0, 1, "up")
                up(n0 + 1, 1, X)
                if not first_block:
                    pe.wait_ge(s_added, SUBS * b)
                else:
                    pe.wait_ge(s_down_lo, HT)
                    pe.wait_ge(s_down_hi, HT)
                slabs(0, 0, 0, "down")
                down(n0, 0, True, False)
                with pe.Fori(1, HT // 2) as jj:
                    for u in range(2):
                        slabs(2 * jj + u, jj, u, "up")
                        pe.wait_ge(s_h, n0 + 2 * jj + u - 1)
                        up(n0 + 2 * jj + u, u, X)
                        v = 1 - u
                        slabs(2 * jj + u - 1, jj - v, v, "down")
                        down(n0 + 2 * jj + u - 1, v, False, False)
                if build:
                    before_build()
                    pe.wait_ge(s_h, n0 + HT - 1)
                    transposes(src, gu, (0, 1))
                    pe.wait_ge(s_h, n0 + HT)
                    transposes(src, gu, (2, 3))
                slabs(HT - 1, HT // 2 - 1, 1, "down")
                down(n0 + HT - 1, 1, False, True)

            def project(m, o, X, s):
                for k in range(KT):
                    ins = products(o, X[:, 0, k, s * P:(s + 1) * P], X[:, 1, k, s * P:(s + 1) * P],
                                   w_attn[:, m, 0, k, :], w_attn[:, m, 1, k, :], k == 0, k == KT - 1)
                return ins

            def qkv(i, X, ln, build, first):
                pe.wait_ge(s_xt_lo, 4 * (build + 1))
                for s in range(SUBS):
                    if s < 2:
                        if not first:
                            pe.wait_ge(s_x2, SUBS * (i - 1) + 2 * s + 2)
                    else:
                        pe.wait_ge(s_rope, SUBS * i + s - 1)
                    for m in (Q, K):
                        ins = project(m, gu[:, 2 * (s % 2) + m, :], X, s)
                    ins.then_inc(s_qk, 1)
                    if s == 1 and not first:
                        pe.wait_ge(s_ln, ln + 1)
                        transposes(lambda t: 12 + t, acc, range(KT))
                for s in range(SUBS):
                    pe.wait_ge(s_rope, SUBS * i + s // 2 + 3)
                    project(V, gu[:, s, :], X, s).then_inc(s_v_ps, 1)

            pe.wait_ge(s_const, 32)
            pe.wait_ge(s_fwht, 1)
            for a in range(HT):
                if a >= 4:
                    pe.wait_ge(s_down_hi, a - 3)
                    pe.wait_ge(s_down_lo, a - 3)
                nc.tensor.matmul(acc[:, a % 4, :], hada[:], tok[:, a, :], start=True, stop=True).then_inc(s_had_ps, 1)
            pe.wait_ge(s_ln, 1)
            for k in range(KT):
                for s in range(SUBS):
                    ins = nc.tensor.transpose(gu[:, k, s * P:(s + 1) * P], x_mid[:, s, k * P:(k + 1) * P], ident[:])
                ins.then_inc(s_xt_ps, 1)
            pe.wait_ge(s_xt_lo, 4)
            ffn(0, xt[0], False, first_block=True)
            pe.wait_ge(s_ln, 2)
            transposes(lambda s: 12 + s, acc, range(KT))
            pe.wait_ge(s_wattn, 4)
            qkv(0, xt[0], None, 1, True)
            pe.wait_ge(s_ln, 3)
            pe.wait_ge(s_v, SUBS)
            transposes(lambda s: 12 + s, gu, range(KT))

            def wo(i, build):
                pe.wait_ge(s_xt_lo, 4 * (build + 1))
                for s in range(SUBS):
                    project(O, gu[:, s, :], xt[1], s).then_inc(s_wo, 1)

            def iteration(i, last):
                e, l = 3 + 4 * (i - 1), 3 + 3 * (i - 1)
                pe.wait_ge(s_xt_lo, 4 * e)
                ffn(2 * i - 1, xt[0], True, lambda: pe.wait_ge(s_attn, SUBS * i), lambda s: 2 * s)
                wo(i, e)
                pe.wait_ge(s_ln, l + 1)
                transposes(lambda s: 12 + s, acc, range(KT))
                qkv(i, xt[0], l + 1, e + 1, False)
                pe.wait_ge(s_xt_lo, 4 * (e + 3))
                pe.wait_ge(s_v, SUBS * (i + 1))
                ffn(2 * i, xt[1], not last, lambda: pe.wait_ge(s_ln, l + 3), lambda s: 12 + s)

            with pe.Fori(1, LAST) as i:
                iteration(i, False)
            iteration(LAST, True)
            e, l = 3 + 4 * LAST - 1, 3 + 3 * LAST - 1
            pe.wait_ge(s_attn, SUBS * TILES)
            pe.wait_ge(s_h, HT * (2 * TILES - 1))
            transposes(lambda s: 2 * s, gu, range(KT))
            wo(TILES, e)
            pe.wait_ge(s_ln, l + 1)
            pe.wait_ge(s_added, SUBS * (2 * TILES - 1))
            transposes(lambda s: 12 + s, acc, range(KT))
            pe.wait_ge(s_xt_lo, 4 * (e + 2))
            pe.wait_ge(s_x2, SUBS * TILES)
            ffn(2 * TILES - 1, xt[1], False)

        @block.scalar
        def _(act):
            def silu(n, u, wait):
                act.wait_ge(s_up_done, n + 1)
                if wait:
                    act.wait_ge(s_hid_lo, n - 1)
                nc.scalar.activation(gated[:, u, :], gu[:, 2 * u, :], ACT.Silu).then_inc(s_silu, 1)

            def hid_high(n, u, wait):
                act.wait_ge(s_h, n + 1)
                if wait:
                    act.wait_ge(s_down_done, n - 1)
                nc.scalar.activation(hid[:, u, 0, :], gated[:, u, :], ACT.Copy).then_inc(s_hid_hi, 1)

            def xt_high(X, bank, build):
                for k in range(KT):
                    act.wait_ge(s_xt_ps, 4 * build + k + 1)
                    nc.scalar.activation(X[:, 0, k, :], bank[:, k, :], ACT.Copy).then_inc(s_xt_hi, 1)

            def ffn(b, attention):
                n0 = HT * b
                if attention is None:
                    with act.Fori(0, HT // 2) as jj:
                        for u in range(2):
                            silu(n0 + 2 * jj + u, u, True)
                            hid_high(n0 + 2 * jj + u, u, True)
                else:
                    with act.Fori(0, 2) as h:
                        for j in range(HT // 2):
                            silu(n0 + 8 * h + j, j % 2, True)
                            hid_high(n0 + 8 * h + j, j % 2, True)
                            if j == HT // 4:
                                exp(attention + h)

            def exp(c):
                act.wait_ge(s_shift, c + 1)
                nc.scalar.activation(scores[:], scores[:], ACT.Exp, scale=SCORE_SCALE).then_inc(s_exp, 1)

            act.wait_ge(s_angle, 1)
            nc.scalar.activation(sin_t[:, 0:POS], sin_t[:, 0:POS], ACT.Sin).then_inc(s_trig, 1)
            nc.scalar.activation(cos_t[:, 0:POS], cos_t[:, 0:POS], ACT.Sin).then_inc(s_trig, 1)
            act.wait_ge(s_trig, 2)
            for r in range(1, B):
                nc.scalar.activation(sin_t[:, r * POS:(r + 1) * POS], sin_t[:, 0:POS], ACT.Copy).then_inc(s_trig, 1)
                nc.scalar.activation(cos_t[:, r * POS:(r + 1) * POS], cos_t[:, 0:POS], ACT.Copy).then_inc(s_trig, 1)
            for a in range(HT):
                act.wait_ge(s_had_ps, a + 1)
                if a >= 2:
                    act.wait_ge(s_down_stored[a % 2], 16 * (a // 2))
                nc.scalar.activation(w_down[:, a % 2, 0, :], acc[:, a % 4, :], ACT.Copy, scale=DOWN_SCALE).then_inc(s_down_hi, 1)
            xt_high(xt[0], gu, 0)

            def up_high(n, jj, u, wait):
                act.wait_ge(s_up_raw[u], 16 * (jj + 1))
                if wait:
                    act.wait_ge(s_up_done, n - 1)
                    act.wait_ge(s_up_stored[u], 16 * jj)
                nc.scalar.activation(w_up[:, u, 0].rearrange("p a b c -> p (a b c)"), prod[:, u, :], ACT.Copy).then_inc(s_up_hi, 1)

            up_high(0, 0, 0, False)
            up_high(1, 0, 1, False)
            for u in range(2):
                silu(u, u, False)
                hid_high(u, u, False)
            with act.Fori(1, HT // 2) as jj:
                for u in range(2):
                    up_high(2 * jj + u, jj, u, True)
                    silu(2 * jj + u, u, True)
                    hid_high(2 * jj + u, u, True)

            def move_x(i):
                act.wait_ge(s_added, SUBS * (2 * i) if not isinstance(i, int) or i > 0 else SUBS)
                act.wait_ge(s_ln, 3 + 3 * (i - 1) + 1 if not isinstance(i, int) or i > 0 else 2)
                if not isinstance(i, int) or i > 0:
                    act.wait_ge(s_x2, SUBS * i)
                nc.scalar.activation(x_mid[:], x_in[:], ACT.Copy).then_inc(s_mid, 1)

            def values(i):
                for s in range(SUBS):
                    act.wait_ge(s_v_ps, SUBS * i + s + 1)
                    nc.scalar.activation(tok[:, 8 + s, :], gu[:, s, :], ACT.Copy).then_inc(s_v, 1)

            xt_high(xt[0], acc, 1)
            move_x(0)
            values(0)
            xt_high(xt[0], gu, 2)
            for c in range(2):
                exp(c)

            def iteration(i, last):
                e = 3 + 4 * (i - 1)
                ffn(2 * i - 1, SUBS * (i - 1) + 2)
                xt_high(xt[1], gu, e)
                xt_high(xt[0], acc, e + 1)
                move_x(i)
                xt_high(xt[1], acc, e + 2)
                values(i)
                ffn(2 * i, SUBS * i)
                if not last:
                    xt_high(xt[0], gu, e + 3)

            with act.Fori(1, LAST) as i:
                iteration(i, False)
            iteration(LAST, True)
            for c in (SUBS * TILES - 2, SUBS * TILES - 1):
                exp(c)
            e = 3 + 4 * LAST - 1
            xt_high(xt[1], gu, e)
            xt_high(xt[1], acc, e + 1)
            ffn(2 * TILES - 1, None)

        @block.gpsimd
        def _(pool):
            nc.gpsimd.memset(minus_half[:], -0.5).then_inc(s_tabs, 1)
            nc.gpsimd.memset(eps[:], EPS).then_inc(s_tabs, 1)
            nc.gpsimd.iota(scores[:].rearrange("p a b -> p (a b)")[:, 0:POS], pattern=[[P, POS]], base=0,
                           channel_multiplier=1, allow_small_or_imprecise_dtypes=True).then_inc(s_tabs, 1)
            pool.wait_ge(s_tabs, 3)

            def inverse_root(l):
                pool.wait_ge(s_var, l + 1)
                nc.gpsimd.tensor_tensor(rstd[:], mean_var[:, :, 1], eps[:], ALU.add).then_inc(s_eps, 1)
                pool.wait_ge(s_eps, l + 1)
                nc.gpsimd.tensor_tensor(rstd[:], rstd[:], minus_half[:], ALU.pow).then_inc(s_rstd, 1)

            inverse_root(0)
            for m in range(4):
                pool.wait_ge(s_attn_raw[m], 16)
                raw = tok[:, 4 * m:4 * m + 4, :]
                nc.gpsimd.tensor_copy(w_attn[:, m, 0], raw).then_inc(s_pool, 1)
                pool.wait_ge(s_pool, m + 1)
                nc.gpsimd.tensor_tensor(w_attn[:, m, 1], raw, w_attn[:, m, 0].bitcast(FP32), ALU.subtract).then_inc(s_wattn, 1)
            with pool.Fori(1, 3 + 3 * LAST) as l:
                inverse_root(l)

        @block.vector
        def _(dve):
            chain = Count(s_dve)

            def link(ins):
                dve.wait_ge(s_dve, chain.mark(ins))

            places = iter(range(1, 64))

            def small_copy():
                at = next(places)
                return nc.vector.tensor_copy(carrier[:, at:at + 1], carrier[:, 0:1])

            def carry(sem, value):
                dve.wait_ge(sem, value)
                small_copy()

            def h_and_low(n, u, wait, between, wait_dve=True):
                dve.wait_ge(s_silu, n + 1)
                nc.vector.tensor_tensor(gated[:, u, :], gated[:, u, :], gu[:, 2 * u + 1, :], ALU.mult).then_inc(s_h, 1)
                between()
                dve.wait_ge(s_hid_hi, n + 1)
                nc.vector.tensor_tensor(hid[:, u, 1, :], gated[:, u, :], hid[:, u, 0, :].bitcast(FP32), ALU.subtract)\
                    .then_inc(s_hid_lo, 1)

            def xt_low(X, bank, build):
                for k in range(KT):
                    dve.wait_ge(s_xt_hi, 4 * build + k + 1)
                    nc.vector.tensor_tensor(X[:, 1, k, :], bank[:, k, :], X[:, 0, k, :].bitcast(FP32), ALU.subtract)\
                        .then_inc(s_xt_lo, 1)

            def l_is_later(l):
                return not isinstance(l, int) or l > 0

            def layer_norm(src, dst, l):
                for s in range(SUBS):
                    at = chain.mark(nc.vector.bn_stats(stats[:, s, :], src[:, s, :]))
                carry(s_dve, at)
                if l_is_later(l):
                    carry(s_ln, l)
                for s in range(SUBS):
                    ins = nc.vector.bn_aggr(mean_var[:, s, :], stats[:, s, :])
                ins.then_inc(s_var, 1)
                dve.wait_ge(s_rstd, l + 1)
                for s in range(SUBS):
                    ins = nc.vector.tensor_scalar(dst(s), src[:, s, :], mean_var[:, s, 0:1], rstd[:, s:s + 1],
                                                  ALU.subtract, ALU.mult)
                ins.then_inc(s_ln, 1)

            def add_sums(b, src, dst):
                dve.wait_ge(s_down_done, HT * (b + 1))
                for s in range(SUBS):
                    ins = nc.vector.tensor_tensor(dst[:, s, :], src[:, s, :], acc[:, s, :], ALU.add)
                    ins.then_inc(s_added, 1)

            def heads(ap):
                return ap.rearrange("p (h d) -> p h d", h=HEADS)

            def tok_at(slot):
                if isinstance(slot, int):
                    return heads(tok[:, slot, :])
                return tok[:, bass.ds(slot, 1), :].rearrange("p o (h d) -> p (o h) d", h=HEADS)

            def qk_piece(s, g, half):
                q, k = tok_at(2 * s), tok_at(2 * s + 1)
                o = prod[:, half, :].rearrange("p (h t d) -> p h t d", h=2, t=HEADS)
                return nc.vector.tensor_tensor(
                    o, wide(q[:, 2 * g:2 * g + 2, None, :], 2, HEADS), wide(k[:, None, :, :], 1, 2), ALU.mult)

            def pv_piece(s, g, half):
                v = tok_at(8 + s)
                o = prod[:, half, :].rearrange("p (h d t) -> p h d t", h=2, d=HD)
                return nc.vector.tensor_tensor(
                    o, wide(scores[:, 2 * g:2 * g + 2, None, :], 2, HD),
                    wide(v.rearrange("p t d -> p d t")[:, None, :, :], 1, 2), ALU.mult)

            def qk_sum(g, half):
                return nc.vector.tensor_reduce(scores[:, 2 * g:2 * g + 2, :],
                                               prod[:, half, :].rearrange("p (h t d) -> p h t d", h=2, t=HEADS), AX.X, ALU.add)

            def pv_sum(s, g, half):
                return nc.vector.tensor_reduce(mixed[:, 2 * g:2 * g + 2, :],
                                               prod[:, half, :].rearrange("p (h d t) -> p h d t", h=2, d=HD), AX.X, ALU.add)

            def shift(last_sum, c):
                dve.wait_ge(s_dve, last_sum)
                link(nc.vector.tensor_reduce(head_max[:], scores[:], AX.X, ALU.max))
                nc.vector.tensor_tensor(scores[:], scores[:], wide(head_max[:, :, None], 2, HEADS), ALU.subtract)\
                    .then_inc(s_shift, 1)

            def row_sums(c):
                dve.wait_ge(s_exp, c + 1)
                dve.wait_ge(s_attn, c)
                link(nc.vector.tensor_reduce(head_sum[:], scores[:], AX.X, ALU.add))
                chain.mark(nc.vector.reciprocal(head_sum[:], head_sum[:]))

            PIECES = HEADS // 2
            CHAIN_SUB = 4 * PIECES + 3

            def attention_sub(s, c, step):
                free = [chain.start + chain.k] * 2
                for j in range(HT // 2):
                    g = 2 * (j % 4)
                    at = []
                    piece = qk_piece if j < 4 else pv_piece

                    def first():
                        dve.wait_ge(s_dve, free[0])
                        at.append(chain.mark(piece(s, g, 0)))

                    if j == HT // 4:
                        step(j, lambda: None)
                        row_sums(c)
                        first()
                    else:
                        step(j, first)
                    dve.wait_ge(s_dve, free[1])
                    at.append(chain.mark(piece(s, g + 1, 1)))
                    for half in range(2):
                        dve.wait_ge(s_dve, at[half])
                        done = free[half] = chain.mark(qk_sum(g + half, half) if j < 4 else pv_sum(s, g + half, half))
                    if j == HT // 4 - 1:
                        shift(done, c)
                    if j == HT // 2 - 1:
                        dve.wait_ge(s_dve, done)
                        nc.vector.tensor_tensor(tok_at(2 * s), mixed[:], wide(head_sum[:, :, None], 2, HD),
                                                ALU.mult).then_inc(s_attn, 1)

            def ffn(b, subs, c):
                n0 = HT * b
                if subs is None:
                    with dve.Fori(0, HT // 2) as jj:
                        for u in range(2):
                            h_and_low(n0 + 2 * jj + u, u, True, lambda: None)
                    return
                start = chain.start + chain.k
                with dve.Fori(0, 2) as h:
                    chain.start, chain.k = start + CHAIN_SUB * h, 0
                    attention_sub(h + subs, c + h, lambda j, between: h_and_low(n0 + 8 * h + j, j % 2, True, between))
                    assert chain.k == CHAIN_SUB, chain.k
                chain.start, chain.k = start + 2 * CHAIN_SUB, 0

            def rope(i, s):
                dve.wait_ge(s_qk, SUBS * i + s + 1)
                src = gu[:, 2 * (s % 2):2 * (s % 2) + 2, :].rearrange("p m (h f e) -> p (m h) f e", h=HEADS, e=2)
                x1, x2 = src[:, :, :, 0], src[:, :, :, 1]
                dst = tok[:, 2 * s:2 * s + 2, :].rearrange("p m (h e f) -> p (m h) e f", h=HEADS, e=2)

                def table(t):
                    if isinstance(i, int):
                        a = t[:, SUBS * i + s:SUBS * i + s + 1, :]
                    else:
                        a = t[:, bass.ds(SUBS * i + s, 1), :]
                    return wide(a, 1, 2 * HEADS)

                def tmp(r, part):
                    return prod[:, r, :].rearrange("p (e h f) -> p e h f", e=2, h=2 * HEADS)[:, part]

                dve.wait_ge(s_dve, chain.start + chain.k)
                at = []
                for r, part, a, t in ((0, 0, x1, cos_t), (0, 1, x2, sin_t), (1, 0, x1, sin_t), (1, 1, x2, cos_t)):
                    ins = nc.vector.tensor_tensor(tmp(r, part), a, table(t), ALU.mult)
                    at.append(chain.mark(ins))
                dve.wait_ge(s_dve, at[1])
                nc.vector.tensor_tensor(dst[:, :, 0, :], tmp(0, 0), tmp(0, 1), ALU.subtract)
                dve.wait_ge(s_dve, at[3])
                link(nc.vector.tensor_tensor(dst[:, :, 1, :], tmp(1, 0), tmp(1, 1), ALU.add))
                small_copy().then_inc(s_rope, 1)

            link(nc.vector.memset(carrier[:, 0:1], 0.0))
            dve.wait_ge(s_x, 16)
            layer_norm(x_in, lambda s: x_mid[:, s, :], 0)
            dve.wait_ge(s_freq_out, 16)
            dve.wait_ge(s_tabs, 3)
            pos = scores[:].rearrange("p a b -> p (a b)")[:, 0:POS]
            angle = gated[:, 0, 0:POS * NF].rearrange("p (a b) -> p a b", a=POS)
            turns = gated[:, 1, 0:POS * NF].rearrange("p (a b) -> p a b", a=POS)
            link(nc.vector.tensor_tensor(angle, wide(pos[:, :, None], 2, NF), wide(freq[:, None, :], 1, POS), ALU.mult))
            MAGIC = 1.5 * 2.0 ** 23
            TWO_PI = 2.0 * np.pi
            C1 = 6.28125
            C2 = float(np.float32(np.round((TWO_PI - C1) * 2.0 ** 21) / 2.0 ** 21))
            C3 = float(np.float32(TWO_PI - C1 - C2))
            LIMIT = float(np.float32(3.1415925))
            for table, quarter in ((sin_t, 0.0), (cos_t, 0.25)):
                r = table[:, 0:POS]
                link(nc.vector.tensor_scalar(turns, angle, float(1.0 / TWO_PI), quarter, ALU.mult, ALU.add))
                link(nc.vector.tensor_scalar(turns, turns, MAGIC, None, ALU.add))
                link(nc.vector.tensor_scalar(turns, turns, MAGIC, None, ALU.subtract))
                link(nc.vector.scalar_tensor_tensor(r, turns, -C1, angle, ALU.mult, ALU.add))
                link(nc.vector.scalar_tensor_tensor(r, turns, -C2, r, ALU.mult, ALU.add))
                link(nc.vector.scalar_tensor_tensor(r, turns, -C3, r, ALU.mult, ALU.add))
                if quarter:
                    link(nc.vector.tensor_scalar(r, r, float(np.pi / 2), None, ALU.add))
                link(nc.vector.tensor_scalar(r, r, LIMIT, -LIMIT, ALU.min, ALU.max))
            small_copy().then_inc(s_angle, 1)
            dve.wait_ge(s_w2, 16)
            for st in (1, 2, 4, 8):
                v = tok[:].rearrange("p (g e t) n -> p g e (t n)", e=2, t=st)
                a, b = v[:, :, 0, :], v[:, :, 1, :]
                link(nc.vector.tensor_tensor(b, a, b, ALU.subtract))
                link(nc.vector.scalar_tensor_tensor(a, a, 2.0, b, ALU.mult, ALU.subtract))
            small_copy().then_inc(s_fwht, 1)
            for a in range(HT):
                dve.wait_ge(s_down_hi, a + 1)
                nc.vector.scalar_tensor_tensor(w_down[:, a % 2, 1, :], acc[:, a % 4, :], DOWN_SCALE,
                                               w_down[:, a % 2, 0, :].bitcast(FP32), ALU.mult, ALU.subtract).then_inc(s_down_lo, 1)
            xt_low(xt[0], gu, 0)

            def up_low(n, u):
                dve.wait_ge(s_up_hi, n + 1)
                nc.vector.tensor_tensor(w_up[:, u, 1].rearrange("p a b c -> p (a b c)"), prod[:, u, :],
                                        w_up[:, u, 0].rearrange("p a b c -> p (a b c)").bitcast(FP32), ALU.subtract).then_inc(s_up_lo, 1)

            up_low(0, 0)
            up_low(1, 1)
            for u in range(2):
                h_and_low(u, u, False, lambda: None)
            with dve.Fori(1, HT // 2) as jj:
                for u in range(2):
                    up_low(2 * jj + u, u)
                    h_and_low(2 * jj + u, u, True, lambda: None)

            normed = lambda s: tok[:, 12 + s, :]
            dve.wait_ge(s_wattn, 4)
            add_sums(0, x_in, x_in)
            dve.wait_ge(s_added, SUBS)
            layer_norm(x_in, normed, 1)
            xt_low(xt[0], acc, 1)
            dve.wait_ge(s_trig, 2 * B)
            for s in range(SUBS):
                rope(0, s)
            dve.wait_ge(s_x, 32)
            layer_norm(x_in, normed, 2)
            xt_low(xt[0], gu, 2)
            dve.wait_ge(s_v, SUBS)
            for s in range(2):
                attention_sub(s, s, lambda j, between: between())

            def after_attention(i, l):
                dve.wait_ge(s_mid, i)
                for s in range(SUBS):
                    dve.wait_ge(s_wo, SUBS * (i - 1) + s + 1)
                    nc.vector.tensor_tensor(x_out[:, s, :], x_mid[:, s, :], gu[:, s, :], ALU.add).then_inc(s_x2, 1)
                dve.wait_ge(s_x2, SUBS * i)
                layer_norm(x_out, normed, l)

            def iteration(i, last):
                e, l = 3 + 4 * (i - 1), 3 + 3 * (i - 1)
                ffn(2 * i - 1, 2, SUBS * (i - 1) + 2)
                xt_low(xt[1], gu, e)
                add_sums(2 * i - 1, x_in, x_in)
                dve.wait_ge(s_added, SUBS * 2 * i)
                layer_norm(x_in, normed, l)
                xt_low(xt[0], acc, e + 1)
                dve.wait_ge(s_freq_out, 16 * i)
                after_attention(i, l + 1)
                rope(i, 0)
                rope(i, 1)
                xt_low(xt[1], acc, e + 2)
                rope(i, 2)
                rope(i, 3)
                if not last:
                    dve.wait_ge(s_x, 16 * (i + 2))
                    layer_norm(x_in, normed, l + 2)
                carry(s_v, SUBS * (i + 1))
                ffn(2 * i, 0, SUBS * i)
                if not last:
                    xt_low(xt[0], gu, e + 3)
                add_sums(2 * i, x_out, x_out)

            start = chain.start + chain.k
            PER = 3 * SUBS + 4 * CHAIN_SUB + 5 * SUBS
            with dve.Fori(1, LAST) as i:
                chain.start, chain.k = start + PER * (i - 1), 0
                iteration(i, False)
            chain.start, chain.k = start + PER * (LAST - 1), 0
            iteration(LAST, True)
            for s in range(2, SUBS):
                attention_sub(s, SUBS * LAST + s, lambda j, between: between())
            e, l = 3 + 4 * LAST - 1, 3 + 3 * LAST - 1
            xt_low(xt[1], gu, e)
            dve.wait_ge(s_freq_out, 16 * TILES)
            after_attention(TILES, l)
            xt_low(xt[1], acc, e + 1)
            ffn(2 * TILES - 1, None, None)
            add_sums(2 * TILES - 1, x_out, x_out)


def hadamard_128():
    h = np.ones((1, 1), np.float32)
    while h.shape[0] < P:
        h = np.block([[h, h], [h, -h]]).astype(np.float32)
    return h


def kernel(L0_attn_x, L0_attn_wq, L0_attn_wk, L0_attn_wv, L0_attn_wo, L0_attn_inv_freq, L0_ffn_W1, L0_ffn_W2, L0_ffn_W3):
    import concourse.bacc as bacc
    from concourse.bass_utils import run_bass_kernel_spmd

    def contraction_major(w, n):
        return np.asarray(w).reshape(-1, n, KT, P).transpose(0, 3, 2, 1)

    w1, w3 = contraction_major(L0_ffn_W1, P), contraction_major(L0_ffn_W3, P)
    arrays = {
        "x": np.asarray(L0_attn_x).reshape(B * S, D),
        "up_raw": np.stack([w1, w3], axis=2).reshape(HT, P, 2 * KT * P),
        "w2t": np.asarray(L0_ffn_W2).T.reshape(HT, P, D),
        "attn_raw": np.stack([contraction_major(w, D)[0] for w in (L0_attn_wq, L0_attn_wk, L0_attn_wv, L0_attn_wo)]),
        "inv_freq": np.asarray(L0_attn_inv_freq),
        "hadamard": hadamard_128(),
        "identity": np.eye(P, dtype=np.float32),
    }
    arrays = {name: np.ascontiguousarray(a) for name, a in arrays.items()}
    nc = bacc.Bacc("TRN2", target_bir_lowering=False, num_devices=1)
    aps = [nc.dram_tensor(name, a.shape, FP32, kind="ExternalInput").ap() for name, a in arrays.items()]
    out = nc.dram_tensor("out", (B * S, D), FP32, kind="ExternalOutput").ap()
    build(nc, *aps, out)
    r = run_bass_kernel_spmd(nc, [arrays], core_ids=[0])
    return r.results[0]["out"].reshape(B, S, D)
```

```python
import itertools
from contextlib import ExitStack

import numpy as np
import concourse.bass as bass
from concourse import mybir

FP32 = mybir.dt.float32
FP32R = mybir.dt.float32r
ALU = mybir.AluOpType
ACT = mybir.ActivationFunctionType
AX = mybir.AxisListType

B, S, D, HID = 4, 1024, 512, 2048
HEADS = 16
HD = D // HEADS
NF = HD // 2
P = 128
TOK = 512
TILES = B * S // TOK
SUBS = TOK // P
KT = D // P
HT = HID // P
POS = S // P
EPS = 1e-5
DOWN_SCALE = 0.5 / float(np.sqrt(HID))
SCORE_SCALE = 1.0 / float(np.sqrt(HD))
Q, K, V, O = range(4)
W2_CUTS = (slice(0, 160), slice(160, 320), slice(320, D))


class Count:

    def __init__(self, sem):
        self.sem, self.start, self.k = sem, 0, 0

    def mark(self, ins):
        ins.then_inc(self.sem, 1)
        self.k += 1
        return self.start + self.k


def wide(ap, dim, n):
    shape = list(ap.shape)
    shape[dim] = n
    return ap.broadcast_to(shape)


def build(nc, x, up_raw, w2t, attn_raw, inv_freq, hadamard, identity, out):
    ctx = ExitStack()
    with ctx:
        def sb(name, shape, dt=FP32):
            return ctx.enter_context(nc.sbuf_tensor(name, shape, dt))

        def sem(name):
            return ctx.enter_context(nc.semaphore(name))

        up_pairs = nc.dram_tensor("up_pairs", [HT, P, 2 * 2 * KT * P], FP32).ap()
        down_pairs = nc.dram_tensor("down_pairs", [HT, P, 2 * D], FP32).ap()

        w_attn = sb("w_attn", [P, 4, 2, KT, D], FP32R)
        w_up = sb("w_up", [P, 2, 2, 2, KT, P], FP32R)
        w_down = sb("w_down", [P, 2, 2, D], FP32R)
        down_stage = w_attn[:].rearrange("p m a k n -> p (m a k n)").rearrange("p (a n) -> p a n", a=HT)
        xt = [sb(f"xt{i}", [P, 2, KT, TOK], FP32R) for i in range(2)]
        hid = sb("hid", [P, 2, 2, TOK], FP32R)
        gated = sb("gated", [P, 2, TOK])
        x_in = sb("x_in", [P, SUBS, D])
        x_mid = sb("x_mid", [P, SUBS, D])
        x_out = sb("x_out", [P, SUBS, D])
        tok = sb("tok", [P, 4 * SUBS, D])
        prod = sb("prod", [P, 3, 2 * HEADS * HD])
        scores = sb("scores", [P, HEADS, HEADS])
        head_max = sb("head_max", [P, HEADS])
        head_sum = sb("head_sum", [P, HEADS])
        cos_t = sb("cos_t", [P, POS, NF])
        sin_t = sb("sin_t", [P, POS, NF])
        ident = sb("ident", [P, P])
        hada = sb("hada", [P, P])
        freq = sb("freq", [P, NF])
        stats = sb("stats", [P, SUBS, 6])
        mean_var = sb("mean_var", [P, SUBS, 2])
        rstd = sb("rstd", [P, SUBS])
        eps = sb("eps", [P, SUBS])
        mixed = sb("mixed", [P, HEADS, HD])
        carrier = sb("carrier", [P, 64])
        minus_half = sb("minus_half", [P, SUBS])

        acc = ctx.enter_context(nc.psum_tensor("acc", [P, SUBS, TOK], FP32))
        gu = ctx.enter_context(nc.psum_tensor("gu", [P, 4, TOK], FP32))

        s_ident = sem("s_ident")
        s_hada = sem("s_hada")
        s_w2 = [sem(f"s_w2_{c}") for c in range(len(W2_CUTS))]
        s_x = sem("s_x")
        s_attn_raw = [sem(f"s_attn_raw{m}") for m in range(4)]
        s_up_raw = [sem(f"s_up_raw{i}") for i in range(2)]
        s_up_loaded = [sem(f"s_up_loaded{i}") for i in range(2)]
        s_down_loaded = [sem(f"s_down_loaded{i}") for i in range(2)]
        s_up_stored = [sem(f"s_up_stored{i}") for i in range(2)]
        s_down_stored = [sem(f"s_down_stored{m}") for m in range(4)]
        s_freq_out = sem("s_freq_out")
        s_tabs = sem("s_tabs")
        s_trig = sem("s_trig")
        s_angle = sem("s_angle")
        s_fwht = sem("s_fwht")
        s_fwht_pool = sem("s_fwht_pool")
        s_had_ps = sem("s_had_ps")
        s_down_hi = sem("s_down_hi")
        s_down_lo = sem("s_down_lo")
        s_up_hi = sem("s_up_hi")
        s_up_lo = sem("s_up_lo")
        s_wo_hi = sem("s_wo_hi")
        s_wattn = sem("s_wattn")
        s_up_done = sem("s_up_done")
        s_silu = sem("s_silu")
        s_h = sem("s_h")
        s_hid_hi = sem("s_hid_hi")
        s_hid_lo = sem("s_hid_lo")
        s_down_done = sem("s_down_done")
        s_added = sem("s_added")
        s_var = sem("s_var")
        s_eps = sem("s_eps")
        s_rstd = sem("s_rstd")
        s_ln = sem("s_ln")
        s_xt_ps = sem("s_xt_ps")
        s_xt_hi = sem("s_xt_hi")
        s_xt_lo = sem("s_xt_lo")
        s_wo = sem("s_wo")
        s_x2 = sem("s_x2")
        s_mid = sem("s_mid")
        s_qk = sem("s_qk")
        s_rope = sem("s_rope")
        s_v_ps = sem("s_v_ps")
        s_v = sem("s_v")
        s_shift = sem("s_shift")
        s_exp = sem("s_exp")
        s_attn = sem("s_attn")
        s_shared = sem("s_shared")
        s_summed = sem("s_summed")
        s_dve = sem("s_dve")
        s_pool = sem("s_pool")

        block = ctx.enter_context(nc.Block())

        LAST = TILES - 1
        def raw_slot(m):
            return 4 * (3 - m)

        EVEN = ((3, 3, 2), (1, 3, 2, 2, 0))
        DENSE = ((4, 4), (4, 4))
        PIECES = HEADS // 2
        POOL_BUFFERS = 3
        SHARED = (1, 2, 3, 5, 6, 7, 10, 11, 13, 14)

        def heads(ap):
            return ap.rearrange("p (h d) -> p h d", h=HEADS)

        def tok_at(slot):
            if isinstance(slot, int):
                return heads(tok[:, slot, :])
            return tok[:, bass.ds(slot, 1), :].rearrange("p o (h d) -> p (o h) d", h=HEADS)

        def product_buffer(b):
            if b < 3:
                return prod[:, b, :]
            return tok[:, 12 + 2 * (b - 3):14 + 2 * (b - 3), :].rearrange("p a n -> p (a n)")

        def unit_products(eng, s, u, buf):
            g = 2 * (u % PIECES)
            if u < PIECES:
                q, k = tok_at(2 * s), tok_at(2 * s + 1)
                return eng.tensor_tensor(product_buffer(buf).rearrange("p (h t d) -> p h t d", h=2, t=HEADS),
                                         wide(q[:, g:g + 2, None, :], 2, HEADS), wide(k[:, None, :, :], 1, 2), ALU.mult)
            v = tok_at(8 + s).rearrange("p t d -> p d t")
            return eng.tensor_tensor(product_buffer(buf).rearrange("p (h d t) -> p h d t", h=2, d=HD),
                                     wide(scores[:, g:g + 2, None, :], 2, HD), wide(v[:, None, :, :], 1, 2), ALU.mult)

        x_v = x.rearrange("(i s p) d -> i p s d", p=P, s=SUBS)
        out_v = out.rearrange("(i s p) d -> i p s d", p=P, s=SUBS)

        @block.sync
        def _(sp):
            def up_slot(u):
                return w_up[:, u].rearrange("p a b c d -> p (a b c d)").bitcast(FP32)

            def down_slot(u):
                return w_down[:, u].rearrange("p a n -> p (a n)").bitcast(FP32)

            def slab(pairs, j):
                return pairs[bass.ds(j, 1)].rearrange("o p n -> p (o n)")

            sp.dma_start(x_in[:], x_v[0]).then_inc(s_x, 16)
            sp.dma_start(ident[:], identity).then_inc(s_ident, 16)
            for j in range(2):
                sp.dma_start(prod[:, j, :], up_raw[j]).then_inc(s_up_raw[j], 16)
            for c in (2, 0, 1):
                sp.dma_start(tok[:, :, W2_CUTS[c]], w2t[:, :, W2_CUTS[c]].rearrange("a p n -> p a n")).then_inc(s_w2[c], 16)
            sp.dma_start(hada[:], hadamard).then_inc(s_hada, 16)
            sp.dma_start(freq[:], wide(inv_freq.rearrange("(a f) -> a f", a=1), 0, P)).then_inc(s_freq_out, 16)

            def keep_up(j, u, more):
                sp.wait_ge(s_up_hi, j + 1)
                sp.wait_ge(s_up_lo, j + 1)
                sp.dma_start(slab(up_pairs, j), up_slot(u)).then_inc(s_up_stored[u], 16)
                if more:
                    sp.dma_start(prod[:, u, :], slab(up_raw, j + 2)).then_inc(s_up_raw[u], 16)

            for j in range(4):
                keep_up(j, j % 2, True)
            for a in range(HT):
                sp.wait_ge(s_down_hi, a + 1)
                sp.wait_ge(s_down_lo, a + 1)
                if a % 4 == 3:
                    m = a // 4
                    sp.dma_start(down_pairs[4 * m:4 * m + 4].rearrange("a p n -> p a n"),
                                 down_stage[:, 4 * m:4 * m + 4, :].bitcast(FP32)).then_inc(s_down_stored[m], 16)
            with sp.Fori(2, 4) as jj:
                for u in range(2):
                    keep_up(2 * jj + u, u, True)
            for m in range(4):
                sp.dma_start(tok[:, raw_slot(m):raw_slot(m) + 4, :], attn_raw[m]).then_inc(s_attn_raw[m], 16)
            with sp.Fori(4, HT // 2 - 1) as jj:
                for u in range(2):
                    keep_up(2 * jj + u, u, True)
            for u in range(2):
                keep_up(HT - 2 + u, u, False)
            for u in range(2):
                sp.wait_ge(s_up_stored[u], 8 * HT)

            def load_up(j, u):
                sp.dma_start(up_slot(u), slab(up_pairs, j)).then_inc(s_up_loaded[u], 16)

            def load_down(j, u):
                sp.dma_start(down_slot(u), slab(down_pairs, j)).then_inc(s_down_loaded[u], 16)

            def weights(b):
                with sp.Fori(0, HT // 2) as jj:
                    for u in range(2):
                        sp.wait_ge(s_up_done, HT * b + 2 * jj + u - 1)
                        load_up(2 * jj + u, u)
                        sp.wait_ge(s_down_done, HT * b + 2 * jj + u - 1)
                        load_down(2 * jj + u, u)

            with sp.Fori(1, 2 * TILES) as b:
                weights(b)

        @block.tensor
        def _(pe):
            def products(o, w_hi, w_lo, m_hi, m_lo, first, last):
                nc.tensor.matmul(o, w_hi, m_hi, start=first, stop=False)
                nc.tensor.matmul(o, w_hi, m_lo, start=False, stop=False)
                return nc.tensor.matmul(o, w_lo, m_hi, start=False, stop=last)

            def xt_ready(build, k, needed=True):
                if needed:
                    pe.wait_ge(s_xt_lo, 4 * build + k + 1)

            def up(n, u, X, build=None):
                for w in range(2):
                    for k in range(KT):
                        xt_ready(build, k, build is not None and w == 0)
                        ins = products(gu[:, 2 * u + w, :], w_up[:, u, 0, w, k, :], w_up[:, u, 1, w, k, :],
                                       X[:, 0, k, :], X[:, 1, k, :], k == 0, k == KT - 1)
                ins.then_inc(s_up_done, 1)

            def down(n, u, first, last, slab=None):
                pe.wait_ge(s_hid_lo, n + 1)
                hi, lo = (w_down[:, u, 0, :], w_down[:, u, 1, :]) if slab is None else slab
                for s in range(SUBS):
                    ins = products(acc[:, s, :], hid[:, u, 0, s * P:(s + 1) * P], hid[:, u, 1, s * P:(s + 1) * P],
                                   hi, lo, first, last)
                ins.then_inc(s_down_done, 1)

            def staged(j):
                if isinstance(j, int):
                    return down_stage[:, j, 0:D], down_stage[:, j, D:2 * D]
                flat = down_stage.rearrange("p a n -> p (a n)")
                return flat[:, bass.ds(j * 2 * D, D)], flat[:, bass.ds(j * 2 * D + D, D)]

            def transposes(src, bank, ks):
                for k in ks:
                    for s in range(SUBS):
                        ins = nc.tensor.transpose(bank[:, k, s * P:(s + 1) * P], tok[:, src(s), k * P:(k + 1) * P], ident[:])
                    ins.then_inc(s_xt_ps, 1)

            def ffn(b, X, x_build, build, before_build=None, src=None):
                n0 = HT * b

                def up_step(jj, u, x_build=None):
                    pe.wait_ge(s_up_loaded[u], 16 * (HT // 2 * (b - 1) + jj + 1))
                    up(n0 + 2 * jj + u, u, X, x_build)

                def down_step(jj, u, first, last):
                    pe.wait_ge(s_down_loaded[u], 16 * (HT // 2 * (b - 1) + jj + 1))
                    down(n0 + 2 * jj + u, u, first, last)

                up_step(0, 0, x_build)
                up_step(0, 1)
                pe.wait_ge(s_added, SUBS * b)
                down_step(0, 0, True, False)
                with pe.Fori(1, HT // 2) as jj:
                    for u in range(2):
                        pe.wait_ge(s_h, n0 + 2 * jj + u - 1)
                        up_step(jj, u)
                        down_step(jj - 1 + u, 1 - u, False, False)
                if build:
                    before_build()
                    pe.wait_ge(s_h, n0 + HT - 1)
                    transposes(src, gu, (0, 1))
                    pe.wait_ge(s_h, n0 + HT)
                    transposes(src, gu, (2, 3))
                down_step(HT // 2 - 1, 1, False, True)

            def block_0(X):
                def up_step(n, u, wait=True):
                    pe.wait_ge(s_up_hi, n + 1)
                    pe.wait_ge(s_up_lo, n + 1)
                    if wait:
                        pe.wait_ge(s_h, n - 1)
                    up(n, u, X)

                for n in range(4):
                    up_step(n, n % 2, n >= 2)
                hadamard_products()
                pe.wait_ge(s_down_lo, HT)
                pe.wait_ge(s_down_hi, HT)
                for n in range(3):
                    down(n, n % 2, n == 0, False, staged(n))
                with pe.Fori(2, HT // 2) as jj:
                    for u in range(2):
                        n = 2 * jj + u
                        up_step(n, u)
                        down(n - 1, 1 - u, False, False, staged(n - 1))
                down(HT - 1, 1, False, True, staged(HT - 1))

            def project(m, o, X, s, build=None):
                for k in range(KT):
                    xt_ready(build, k, build is not None)
                    ins = products(o, X[:, 0, k, s * P:(s + 1) * P], X[:, 1, k, s * P:(s + 1) * P],
                                   w_attn[:, m, 0, k, :], w_attn[:, m, 1, k, :], k == 0, k == KT - 1)
                return ins

            def qkv(i, X, ln, build, first):
                for s in range(SUBS):
                    if s < 2:
                        if not first:
                            pe.wait_ge(s_x2, SUBS * (i - 1) + 2 * s + 2)
                    else:
                        pe.wait_ge(s_rope, SUBS * i + s - 1)
                    for m in (Q, K):
                        ins = project(m, gu[:, 2 * (s % 2) + m, :], X, s, build if (s, m) == (0, Q) else None)
                    ins.then_inc(s_qk, 1)
                    if s == 1 and not first:
                        pe.wait_ge(s_ln, ln + 1)
                        transposes(lambda t: 12 + t, acc, range(KT))
                for s in range(SUBS):
                    pe.wait_ge(s_rope, SUBS * i + s // 2 + 3)
                    project(V, gu[:, s, :], X, s).then_inc(s_v_ps, 1)

            def hadamard_products():
                pe.wait_ge(s_hada, 16)
                pe.wait_ge(s_fwht, 1)
                pe.wait_ge(s_fwht_pool, 1)
                for a in range(HT):
                    if a >= 4:
                        pe.wait_ge(s_down_hi, a - 3)
                        pe.wait_ge(s_down_lo, a - 3)
                    nc.tensor.matmul(acc[:, a % 4, :], hada[:], tok[:, a, :], start=True, stop=True).then_inc(s_had_ps, 1)

            pe.wait_ge(s_ident, 16)
            pe.wait_ge(s_ln, 1)
            for k in range(KT):
                for s in range(SUBS):
                    ins = nc.tensor.transpose(gu[:, k, s * P:(s + 1) * P], x_mid[:, s, k * P:(k + 1) * P], ident[:])
                ins.then_inc(s_xt_ps, 1)
            pe.wait_ge(s_xt_lo, 4)
            block_0(xt[0])
            pe.wait_ge(s_ln, 2)
            transposes(lambda s: 12 + s, acc, range(KT))
            pe.wait_ge(s_wattn, 3)
            qkv(0, xt[0], None, 1, True)
            pe.wait_ge(s_ln, 3)
            pe.wait_ge(s_v, SUBS)
            transposes(lambda s: 12 + s, gu, range(KT))

            def wo(i, build):
                for s in range(SUBS):
                    if s < 2:
                        xt_ready(build, 2 * s + 1)
                    project(O, gu[:, s, :], xt[1], s, build if s == 0 else None).then_inc(s_wo, 1)

            def iteration(i, last):
                e, l = 3 + 4 * (i - 1), 3 + 3 * (i - 1)
                ffn(2 * i - 1, xt[0], e - 1, True, lambda: pe.wait_ge(s_attn, SUBS * i), lambda s: 2 * s)
                wo(i, e)
                pe.wait_ge(s_ln, l + 1)
                transposes(lambda s: 12 + s, acc, range(KT))
                qkv(i, xt[0], l + 1, e + 1, False)
                pe.wait_ge(s_v, SUBS * (i + 1))
                if last:
                    ffn(2 * i, xt[1], e + 2, True, lambda: pe.wait_ge(s_attn, SUBS * TILES), lambda s: 2 * s)
                else:
                    ffn(2 * i, xt[1], e + 2, True, lambda: pe.wait_ge(s_ln, l + 3), lambda s: 12 + s)

            with pe.Fori(1, LAST) as i:
                iteration(i, False)
            iteration(LAST, True)
            e, l = 3 + 4 * LAST - 1, 3 + 3 * LAST - 1
            wo(TILES, e)
            pe.wait_ge(s_ln, l + 1)
            pe.wait_ge(s_added, SUBS * (2 * TILES - 1))
            transposes(lambda s: 12 + s, acc, range(KT))
            pe.wait_ge(s_x2, SUBS * TILES)
            ffn(2 * TILES - 1, xt[1], e + 1, False)

        @block.scalar
        def _(act):
            def silu(n, u, wait):
                act.wait_ge(s_up_done, n + 1)
                if wait:
                    act.wait_ge(s_hid_lo, n - 1)
                nc.scalar.activation(gated[:, u, :], gu[:, 2 * u, :], ACT.Silu).then_inc(s_silu, 1)

            def hid_high(n, u, wait):
                act.wait_ge(s_h, n + 1)
                if wait:
                    act.wait_ge(s_down_done, n - 1)
                nc.scalar.activation(hid[:, u, 0, :], gated[:, u, :], ACT.Copy).then_inc(s_hid_hi, 1)

            def xt_high(X, bank, build):
                for k in range(KT):
                    act.wait_ge(s_xt_ps, 4 * build + k + 1)
                    nc.scalar.activation(X[:, 0, k, :], bank[:, k, :], ACT.Copy).then_inc(s_xt_hi, 1)

            def ffn(b, attention, plan=EVEN):
                n0 = HT * b
                if attention is None:
                    with act.Fori(0, HT // 2) as jj:
                        for u in range(2):
                            silu(n0 + 2 * jj + u, u, True)
                            hid_high(n0 + 2 * jj + u, u, True)
                else:
                    steps = len(plan[0]) + len(plan[1])
                    with act.Fori(0, HT // steps) as h:
                        for j in range(steps):
                            silu(n0 + steps * h + j, j % 2, True)
                            hid_high(n0 + steps * h + j, j % 2, True)
                            if j == len(plan[0]):
                                exp(attention + h)

            def exp(c):
                act.wait_ge(s_shift, c + 1)
                nc.scalar.activation(scores[:], scores[:], ACT.Exp, scale=SCORE_SCALE).then_inc(s_exp, 1)

            xt_high(xt[0], gu, 0)

            def up_high(n, jj, u, wait):
                act.wait_ge(s_up_raw[u], 16 * (jj + 1))
                if wait:
                    act.wait_ge(s_up_done, n - 1)
                    act.wait_ge(s_up_stored[u], 16 * jj)
                nc.scalar.activation(w_up[:, u, 0].rearrange("p a b c -> p (a b c)"), prod[:, u, :], ACT.Copy).then_inc(s_up_hi, 1)

            def ffn_step(n, u, wait):
                silu(n, u, wait)
                hid_high(n, u, wait)

            up_high(0, 0, 0, False)
            up_high(1, 0, 1, False)
            for u in range(2):
                ffn_step(u, u, False)
                up_high(u + 2, 1, u, True)
            for u in range(2):
                silu(u + 2, u, True)
            for a in range(HT):
                act.wait_ge(s_had_ps, a + 1)
                nc.scalar.activation(down_stage[:, a, 0:D], acc[:, a % 4, :], ACT.Copy, scale=DOWN_SCALE).then_inc(s_down_hi, 1)
            for u in range(2):
                hid_high(u + 2, u, True)
                up_high(u + 4, 2, u, True)
            act.wait_ge(s_angle, 1)
            nc.scalar.activation(sin_t[:, 0:POS], sin_t[:, 0:POS], ACT.Sin).then_inc(s_trig, 1)
            nc.scalar.activation(cos_t[:, 0:POS], cos_t[:, 0:POS], ACT.Sin).then_inc(s_trig, 1)
            with act.Fori(2, HT // 2 - 1) as jj:
                for u in range(2):
                    ffn_step(2 * jj + u, u, True)
                    up_high(2 * jj + u + 2, jj + 1, u, True)
            for u in range(2):
                ffn_step(HT - 2 + u, u, True)
            act.wait_ge(s_attn_raw[O], 16)
            act.wait_ge(s_down_stored[O], 16)
            act.wait_ge(s_down_done, HT)
            nc.scalar.activation(w_attn[:, O, 0], tok[:, raw_slot(O):raw_slot(O) + 4, :], ACT.Copy).then_inc(s_wo_hi, 1)

            def move_x(i):
                act.wait_ge(s_added, SUBS * (2 * i) if not isinstance(i, int) or i > 0 else SUBS)
                act.wait_ge(s_ln, 3 + 3 * (i - 1) + 1 if not isinstance(i, int) or i > 0 else 2)
                if not isinstance(i, int) or i > 0:
                    act.wait_ge(s_x2, SUBS * i)
                nc.scalar.activation(x_mid[:], x_in[:], ACT.Copy).then_inc(s_mid, 1)

            def load_x(i):
                act.wait_ge(s_mid, i)
                act.dma_start(x_in[:], x_v[i] if isinstance(i, int) else
                              x_v[bass.ds(i, 1)].rearrange("o p s d -> p (o s) d")).then_inc(s_x, 16)

            def store_out(i):
                act.wait_ge(s_added, SUBS * (2 * i + 3))
                act.dma_start(out_v[i] if isinstance(i, int) else
                              out_v[bass.ds(i, 1)].rearrange("o p s d -> p (o s) d"), x_out[:]).then_inc(s_freq_out, 16)

            def values(i):
                for s in range(SUBS):
                    act.wait_ge(s_v_ps, SUBS * i + s + 1)
                    nc.scalar.activation(tok[:, 8 + s, :], gu[:, s, :], ACT.Copy).then_inc(s_v, 1)

            xt_high(xt[0], acc, 1)
            move_x(0)
            load_x(1)
            values(0)
            xt_high(xt[0], gu, 2)

            def iteration(i, first, last):
                e = 3 + 4 * (i - 1)
                if first:
                    ffn(1, 0, DENSE)
                else:
                    ffn(2 * i - 1, SUBS * (i - 1) + 2)
                xt_high(xt[1], gu, e)
                xt_high(xt[0], acc, e + 1)
                move_x(i)
                if not last:
                    load_x(i + 1)
                xt_high(xt[1], acc, e + 2)
                values(i)
                if last:
                    ffn(2 * i, SUBS * i, DENSE)
                    xt_high(xt[1], gu, e + 3)
                else:
                    ffn(2 * i, SUBS * i)
                    xt_high(xt[0], gu, e + 3)
                store_out(i - 1)

            iteration(1, True, False)
            with act.Fori(2, LAST) as i:
                iteration(i, False, False)
            iteration(LAST, False, True)
            xt_high(xt[1], acc, 3 + 4 * LAST)
            ffn(2 * TILES - 1, None)
            for s in range(SUBS):
                act.wait_ge(s_added, SUBS * (2 * TILES - 1) + s + 1)
                act.dma_start(out_v[LAST][:, s, :], x_out[:, s, :]).then_inc(s_freq_out, 16)
            act.wait_ge(s_freq_out, 16 * (TILES + SUBS))

        @block.gpsimd
        def _(pool):
            nc.gpsimd.memset(minus_half[:], -0.5).then_inc(s_tabs, 1)
            nc.gpsimd.memset(eps[:], EPS).then_inc(s_tabs, 1)
            nc.gpsimd.iota(scores[:].rearrange("p a b -> p (a b)")[:, 0:POS], pattern=[[P, POS]], base=0,
                           channel_multiplier=1, allow_small_or_imprecise_dtypes=True).then_inc(s_tabs, 1)
            pool.wait_ge(s_tabs, 3)

            def inverse_root(l):
                pool.wait_ge(s_var, l + 1)
                nc.gpsimd.tensor_tensor(rstd[:], mean_var[:, :, 1], eps[:], ALU.add).then_inc(s_eps, 1)
                pool.wait_ge(s_eps, l + 1)
                nc.gpsimd.tensor_tensor(rstd[:], rstd[:], minus_half[:], ALU.pow).then_inc(s_rstd, 1)

            inverse_root(0)
            width = W2_CUTS[-1].stop - W2_CUTS[-1].start
            pool.wait_ge(s_w2[-1], 16)
            sums = x_out[:].rearrange("p s n -> p (s n)")[:, 0:HT // 2 * width].rearrange("p (t n) -> p t n", n=width)
            steps = 0
            for st in (1, 2, 4, 8):
                v = tok[:, :, W2_CUTS[-1]].rearrange("p (g e t) n -> p g e t n", e=2, t=st)
                a, b = v[:, :, 0], v[:, :, 1]
                both = sums.rearrange("p (g t) n -> p g t n", t=st)
                nc.gpsimd.tensor_tensor(both, a, b, ALU.add).then_inc(s_pool, 1)
                nc.gpsimd.tensor_tensor(b, a, b, ALU.subtract).then_inc(s_pool, 1)
                pool.wait_ge(s_pool, steps + 2)
                nc.gpsimd.tensor_copy(a, both).then_inc(s_pool, 1)
                steps += 3
                pool.wait_ge(s_pool, steps)
            nc.gpsimd.memset(eps[:], EPS).then_inc(s_fwht_pool, 1)
            for m in range(4):
                if m == O:
                    inverse_root(1)
                pool.wait_ge(s_attn_raw[m], 16)
                pool.wait_ge(s_down_stored[m], 16)
                pool.wait_ge(s_down_done, 4 * (m + 1))
                raw = tok[:, raw_slot(m):raw_slot(m) + 4, :]
                if m == O:
                    pool.wait_ge(s_wo_hi, 1)
                else:
                    nc.gpsimd.tensor_copy(w_attn[:, m, 0], raw).then_inc(s_pool, 1)
                    pool.wait_ge(s_pool, steps + m + 1)
                nc.gpsimd.tensor_tensor(w_attn[:, m, 1], raw, w_attn[:, m, 0].bitcast(FP32), ALU.subtract).then_inc(s_wattn, 1)

            def shared_products(i, k, last_build):
                pool.wait_ge(s_xt_ps, 4 * (last_build + 1))
                for s in range(SUBS):
                    for u in SHARED:
                        if u < PIECES:
                            pool.wait_ge(s_rope, SUBS * i + s + 1)
                        else:
                            pool.wait_ge(s_exp, SUBS * i + s + 1)
                        if k >= POOL_BUFFERS:
                            pool.wait_ge(s_summed, k - POOL_BUFFERS + 1)
                        unit_products(nc.gpsimd, s, u, 2 + k % POOL_BUFFERS).then_inc(s_shared, 1)
                        k += 1
                return k

            inverse_root(2)
            shared = shared_products(0, 0, 2)
            with pool.Fori(3, 2 + 3 * LAST) as l:
                inverse_root(l)
            shared_products(LAST, shared, 3 + 4 * (LAST - 1) + 2)
            inverse_root(2 + 3 * LAST)

        @block.vector
        def _(dve):
            chain = Count(s_dve)

            def link(ins):
                dve.wait_ge(s_dve, chain.mark(ins))

            places = iter(range(1, 64))

            def small_copy():
                at = next(places)
                return nc.vector.tensor_copy(carrier[:, at:at + 1], carrier[:, 0:1])

            def carry(sem, value):
                dve.wait_ge(sem, value)
                small_copy()

            def h_and_low(n, u, between):
                dve.wait_ge(s_silu, n + 1)
                nc.vector.tensor_tensor(gated[:, u, :], gated[:, u, :], gu[:, 2 * u + 1, :], ALU.mult).then_inc(s_h, 1)
                between()
                dve.wait_ge(s_hid_hi, n + 1)
                nc.vector.tensor_tensor(hid[:, u, 1, :], gated[:, u, :], hid[:, u, 0, :].bitcast(FP32), ALU.subtract)\
                    .then_inc(s_hid_lo, 1)

            def xt_low(X, bank, build):
                for k in range(KT):
                    dve.wait_ge(s_xt_hi, 4 * build + k + 1)
                    nc.vector.tensor_tensor(X[:, 1, k, :], bank[:, k, :], X[:, 0, k, :].bitcast(FP32), ALU.subtract)\
                        .then_inc(s_xt_lo, 1)

            def l_is_later(l):
                return not isinstance(l, int) or l > 0

            def layer_norm(src, dst, l):
                for s in range(SUBS):
                    at = chain.mark(nc.vector.bn_stats(stats[:, s, :], src[:, s, :]))
                carry(s_dve, at)
                if l_is_later(l):
                    carry(s_ln, l)
                for s in range(SUBS):
                    ins = nc.vector.bn_aggr(mean_var[:, s, :], stats[:, s, :])
                ins.then_inc(s_var, 1)
                dve.wait_ge(s_rstd, l + 1)
                for s in range(SUBS):
                    ins = nc.vector.tensor_scalar(dst(s), src[:, s, :], mean_var[:, s, 0:1], rstd[:, s:s + 1],
                                                  ALU.subtract, ALU.mult)
                ins.then_inc(s_ln, 1)

            def add_sums(b, x):
                dve.wait_ge(s_down_done, HT * (b + 1))
                for s in range(SUBS):
                    nc.vector.tensor_tensor(x[:, s, :], x[:, s, :], acc[:, s, :], ALU.add).then_inc(s_added, 1)

            def unit_sum(u, buf):
                g = 2 * (u % PIECES)
                if u < PIECES:
                    return nc.vector.tensor_reduce(scores[:, g:g + 2, :],
                                                   product_buffer(buf).rearrange("p (h t d) -> p h t d", h=2, t=HEADS), AX.X, ALU.add)
                return nc.vector.tensor_reduce(mixed[:, g:g + 2, :],
                                               product_buffer(buf).rearrange("p (h d t) -> p h d t", h=2, d=HD), AX.X, ALU.add)

            def shift(last_sum, c):
                dve.wait_ge(*last_sum)
                link(nc.vector.tensor_reduce(head_max[:], scores[:], AX.X, ALU.max))
                nc.vector.tensor_tensor(scores[:], scores[:], wide(head_max[:, :, None], 2, HEADS), ALU.subtract)\
                    .then_inc(s_shift, 1)

            def row_sums(c):
                dve.wait_ge(s_exp, c + 1)
                dve.wait_ge(s_attn, c)
                link(nc.vector.tensor_reduce(head_sum[:], scores[:], AX.X, ALU.add))
                chain.mark(nc.vector.reciprocal(head_sum[:], head_sum[:]))

            CHAIN_SUB = 4 * PIECES + 3
            taken = itertools.count()
            pooled = itertools.count(1)

            def attention_sub(s, c, plan, step, shared=()):
                free = [chain.start + chain.k] * 2
                made = []
                units = iter(range(2 * PIECES))
                buffers = itertools.cycle((0, 1))

                def products_of(u):
                    if u in shared:
                        made.append((u, 2 + next(taken) % POOL_BUFFERS, None))
                        return
                    buf = next(buffers)
                    dve.wait_ge(s_dve, free[buf])
                    made.append((u, buf, chain.mark(unit_products(nc.vector, s, u, buf))))

                def sum_of_oldest():
                    u, buf, at = made.pop(0)
                    if u in shared:
                        n = next(pooled)
                        dve.wait_ge(s_shared, n)
                        unit_sum(u, buf).then_inc(s_summed, 1)
                        return s_summed, n
                    dve.wait_ge(s_dve, at)
                    free[buf] = chain.mark(unit_sum(u, buf))
                    return s_dve, free[buf]

                for j, n in enumerate(plan[0] + plan[1]):
                    scored = j == len(plan[0])
                    mine = [next(units) for _ in range(n)]
                    if scored:
                        step(j, lambda: None)
                        row_sums(c)
                    else:
                        def between():
                            if mine:
                                shared_unit = mine[0] in shared
                                products_of(mine.pop(0))
                                if shared_unit:
                                    sum_of_oldest()
                        step(j, between)
                    if mine and (made or scored):
                        products_of(mine.pop(0))
                    while made:
                        done = sum_of_oldest()
                        if mine:
                            products_of(mine.pop(0))
                    if j == len(plan[0]) - 1:
                        shift(done, c)
                assert next(units, None) is None
                dve.wait_ge(*done)
                nc.vector.tensor_tensor(tok_at(2 * s), mixed[:], wide(head_sum[:, :, None], 2, HD), ALU.mult).then_inc(s_attn, 1)

            def ffn(b, first_sub, c, plan=EVEN):
                n0 = HT * b
                if first_sub is None:
                    with dve.Fori(0, HT // 2) as jj:
                        for u in range(2):
                            h_and_low(n0 + 2 * jj + u, u, lambda: None)
                    return
                steps = len(plan[0]) + len(plan[1])
                if plan is DENSE:
                    for h in range(SUBS):
                        attention_sub(first_sub + h, c + h, plan,
                                      lambda j, between: h_and_low(n0 + steps * h + j, j % 2, between), SHARED)
                    return
                start = chain.start + chain.k
                with dve.Fori(0, HT // steps) as h:
                    chain.start, chain.k = start + CHAIN_SUB * h, 0
                    attention_sub(h + first_sub, c + h, plan,
                                  lambda j, between: h_and_low(n0 + steps * h + j, j % 2, between))
                    assert chain.k == CHAIN_SUB, chain.k
                chain.start, chain.k = start + HT // steps * CHAIN_SUB, 0

            def rope(i, s):
                dve.wait_ge(s_qk, SUBS * i + s + 1)
                src = gu[:, 2 * (s % 2):2 * (s % 2) + 2, :].rearrange("p m (h f e) -> p (m h) f e", h=HEADS, e=2)
                x1, x2 = src[:, :, :, 0], src[:, :, :, 1]
                dst = tok[:, 2 * s:2 * s + 2, :].rearrange("p m (h e f) -> p (m h) e f", h=HEADS, e=2)

                def table(t):
                    at = (SUBS * i + s) % POS
                    a = t[:, at:at + 1, :] if isinstance(i, int) else t[:, bass.ds(at, 1), :]
                    return wide(a, 1, 2 * HEADS)

                def tmp(r, part):
                    return prod[:, r, :].rearrange("p (e h f) -> p e h f", e=2, h=2 * HEADS)[:, part]

                dve.wait_ge(s_dve, chain.start + chain.k)
                at = []
                for r, part, a, t in ((0, 0, x1, cos_t), (0, 1, x2, sin_t), (1, 0, x1, sin_t), (1, 1, x2, cos_t)):
                    ins = nc.vector.tensor_tensor(tmp(r, part), a, table(t), ALU.mult)
                    at.append(chain.mark(ins))
                dve.wait_ge(s_dve, at[1])
                nc.vector.tensor_tensor(dst[:, :, 0, :], tmp(0, 0), tmp(0, 1), ALU.subtract)
                dve.wait_ge(s_dve, at[3])
                link(nc.vector.tensor_tensor(dst[:, :, 1, :], tmp(1, 0), tmp(1, 1), ALU.add))
                small_copy().then_inc(s_rope, 1)

            def up_low(n, u):
                dve.wait_ge(s_up_hi, n + 1)
                nc.vector.tensor_tensor(w_up[:, u, 1].rearrange("p a b c -> p (a b c)"), prod[:, u, :],
                                        w_up[:, u, 0].rearrange("p a b c -> p (a b c)").bitcast(FP32), ALU.subtract).then_inc(s_up_lo, 1)

            link(nc.vector.memset(carrier[:, 0:1], 0.0))
            dve.wait_ge(s_x, 16)
            layer_norm(x_in, lambda s: x_mid[:, s, :], 0)
            up_low(0, 0)
            xt_low(xt[0], gu, 0)
            up_low(1, 1)
            for c in range(2):
                dve.wait_ge(s_w2[c], 16)
                for st in (1, 2, 4, 8):
                    v = tok[:, :, W2_CUTS[c]].rearrange("p (g e t) n -> p g e t n", e=2, t=st)
                    a, b = v[:, :, 0], v[:, :, 1]
                    link(nc.vector.tensor_tensor(b, a, b, ALU.subtract))
                    if st == 1:
                        pairs = [(a[:, :, 0], b[:, :, 0])]
                    else:
                        pairs = [(a[:, g], b[:, g]) for g in range(HT // (2 * st))]
                    for pa, pb in pairs:
                        at = chain.mark(nc.vector.scalar_tensor_tensor(pa, pa, 2.0, pb, ALU.mult, ALU.subtract))
                    dve.wait_ge(s_dve, at)
                if c == 1:
                    small_copy().then_inc(s_fwht, 1)
                h_and_low(c, c, lambda: None)
                up_low(c + 2, c)
            for a in range(HT):
                dve.wait_ge(s_down_hi, a + 1)
                nc.vector.scalar_tensor_tensor(down_stage[:, a, D:2 * D], acc[:, a % 4, :], DOWN_SCALE,
                                               down_stage[:, a, 0:D].bitcast(FP32), ALU.mult, ALU.subtract).then_inc(s_down_lo, 1)
            for u in range(2):
                h_and_low(u + 2, u, lambda: None)
                up_low(u + 4, u)
            dve.wait_ge(s_freq_out, 16)
            dve.wait_ge(s_tabs, 3)
            pos = scores[:].rearrange("p a b -> p (a b)")[:, 0:POS]
            spare = mixed[:].rearrange("p a b -> p (a b)")
            angle = spare[:, 0:POS * NF].rearrange("p (a b) -> p a b", a=POS)
            turns = spare[:, POS * NF:2 * POS * NF].rearrange("p (a b) -> p a b", a=POS)
            link(nc.vector.tensor_tensor(angle, wide(pos[:, :, None], 2, NF), wide(freq[:, None, :], 1, POS), ALU.mult))
            MAGIC = 1.5 * 2.0 ** 23
            TWO_PI = 2.0 * np.pi
            C1 = 6.28125
            C2 = float(np.float32(np.round((TWO_PI - C1) * 2.0 ** 21) / 2.0 ** 21))
            C3 = float(np.float32(TWO_PI - C1 - C2))
            LIMIT = float(np.float32(3.1415925))
            for table, quarter in ((sin_t, 0.0), (cos_t, 0.25)):
                r = table[:, 0:POS]
                link(nc.vector.tensor_scalar(turns, angle, float(1.0 / TWO_PI), quarter, ALU.mult, ALU.add))
                link(nc.vector.tensor_scalar(turns, turns, MAGIC, None, ALU.add))
                link(nc.vector.tensor_scalar(turns, turns, MAGIC, None, ALU.subtract))
                link(nc.vector.scalar_tensor_tensor(r, turns, -C1, angle, ALU.mult, ALU.add))
                link(nc.vector.scalar_tensor_tensor(r, turns, -C2, r, ALU.mult, ALU.add))
                link(nc.vector.scalar_tensor_tensor(r, turns, -C3, r, ALU.mult, ALU.add))
                if quarter:
                    link(nc.vector.tensor_scalar(r, r, float(np.pi / 2), None, ALU.add))
                link(nc.vector.tensor_scalar(r, r, LIMIT, -LIMIT, ALU.min, ALU.max))
            small_copy().then_inc(s_angle, 1)
            with dve.Fori(2, HT // 2 - 1) as jj:
                for u in range(2):
                    h_and_low(2 * jj + u, u, lambda: None)
                    up_low(2 * jj + u + 2, u)
            for u in range(2):
                h_and_low(HT - 2 + u, u, lambda: None)

            def normed(s):
                return tok[:, 12 + s, :]

            add_sums(0, x_in)
            dve.wait_ge(s_wattn, 1)
            dve.wait_ge(s_added, SUBS)
            layer_norm(x_in, normed, 1)
            xt_low(xt[0], acc, 1)
            dve.wait_ge(s_trig, 2)
            dve.wait_ge(s_wattn, 4)
            for s in range(SUBS):
                rope(0, s)
            dve.wait_ge(s_x, 32)
            layer_norm(x_in, normed, 2)
            xt_low(xt[0], gu, 2)
            carry(s_v, SUBS)

            def after_attention(i, l):
                dve.wait_ge(s_mid, i)
                for s in range(SUBS):
                    dve.wait_ge(s_wo, SUBS * (i - 1) + s + 1)
                    nc.vector.tensor_tensor(x_out[:, s, :], x_mid[:, s, :], gu[:, s, :], ALU.add).then_inc(s_x2, 1)
                dve.wait_ge(s_x2, SUBS * i)
                layer_norm(x_out, normed, l)

            def iteration(i, first, last):
                e, l = 3 + 4 * (i - 1), 3 + 3 * (i - 1)
                if first:
                    ffn(1, 0, 0, DENSE)
                else:
                    ffn(2 * i - 1, 2, SUBS * (i - 1) + 2)
                xt_low(xt[1], gu, e)
                add_sums(2 * i - 1, x_in)
                dve.wait_ge(s_added, SUBS * 2 * i)
                layer_norm(x_in, normed, l)
                xt_low(xt[0], acc, e + 1)
                dve.wait_ge(s_freq_out, 16 * i)
                after_attention(i, l + 1)
                rope(i, 0)
                rope(i, 1)
                xt_low(xt[1], acc, e + 2)
                rope(i, 2)
                rope(i, 3)
                if not last:
                    dve.wait_ge(s_x, 16 * (i + 2))
                    layer_norm(x_in, normed, l + 2)
                carry(s_v, SUBS * (i + 1))
                if last:
                    ffn(2 * i, 0, SUBS * i, DENSE)
                    xt_low(xt[1], gu, e + 3)
                else:
                    ffn(2 * i, 0, SUBS * i)
                    xt_low(xt[0], gu, e + 3)
                add_sums(2 * i, x_out)

            iteration(1, True, False)
            start = chain.start + chain.k
            PER = 3 * SUBS + 4 * CHAIN_SUB + 5 * SUBS
            with dve.Fori(2, LAST) as i:
                chain.start, chain.k = start + PER * (i - 2), 0
                iteration(i, False, False)
            chain.start, chain.k = start + PER * (LAST - 2), 0
            iteration(LAST, False, True)
            dve.wait_ge(s_freq_out, 16 * TILES)
            after_attention(TILES, 3 + 3 * LAST - 1)
            xt_low(xt[1], acc, 3 + 4 * LAST)
            ffn(2 * TILES - 1, None, None)
            add_sums(2 * TILES - 1, x_out)


def hadamard_128():
    h = np.ones((1, 1), np.float32)
    while h.shape[0] < P:
        h = np.block([[h, h], [h, -h]]).astype(np.float32)
    return h


def kernel(L0_attn_x, L0_attn_wq, L0_attn_wk, L0_attn_wv, L0_attn_wo, L0_attn_inv_freq, L0_ffn_W1, L0_ffn_W2, L0_ffn_W3):
    import concourse.bacc as bacc
    from concourse.bass_utils import run_bass_kernel_spmd

    def contraction_major(w, n):
        return np.asarray(w).reshape(-1, n, KT, P).transpose(0, 3, 2, 1)

    w1, w3 = contraction_major(L0_ffn_W1, P), contraction_major(L0_ffn_W3, P)
    arrays = {
        "x": np.asarray(L0_attn_x).reshape(B * S, D),
        "up_raw": np.stack([w1, w3], axis=2).reshape(HT, P, 2 * KT * P),
        "w2t": np.asarray(L0_ffn_W2).T.reshape(HT, P, D),
        "attn_raw": np.stack([contraction_major(w, D)[0] for w in (L0_attn_wq, L0_attn_wk, L0_attn_wv, L0_attn_wo)]),
        "inv_freq": np.asarray(L0_attn_inv_freq),
        "hadamard": hadamard_128(),
        "identity": np.eye(P, dtype=np.float32),
    }
    arrays = {name: np.ascontiguousarray(a) for name, a in arrays.items()}
    nc = bacc.Bacc("TRN2", target_bir_lowering=False, num_devices=1)
    aps = [nc.dram_tensor(name, a.shape, FP32, kind="ExternalInput").ap() for name, a in arrays.items()]
    out = nc.dram_tensor("out", (B * S, D), FP32, kind="ExternalOutput").ap()
    build(nc, *aps, out)
    r = run_bass_kernel_spmd(nc, [arrays], core_ids=[0])
    return r.results[0]["out"].reshape(B, S, D)
```

```python
import itertools
from contextlib import ExitStack

import numpy as np
import concourse.bass as bass
from concourse import mybir

FP32 = mybir.dt.float32
FP32R = mybir.dt.float32r
ALU = mybir.AluOpType
ACT = mybir.ActivationFunctionType
AX = mybir.AxisListType

B, S, D, HID = 4, 1024, 512, 2048
HEADS = 16
HD = D // HEADS
NF = HD // 2
P = 128
TOK = 512
TILES = B * S // TOK
SUBS = TOK // P
KT = D // P
HT = HID // P
POS = S // P
EPS = 1e-5
DOWN_SCALE = 0.5 / float(np.sqrt(HID))
SCORE_SCALE = 1.0 / float(np.sqrt(HD))
Q, K, V, O = range(4)
W2_CUTS = (slice(0, 168), slice(168, 336), slice(336, D))
PARTS = (slice(0, W2_CUTS[1].stop), W2_CUTS[2])


class Count:

    def __init__(self, sem):
        self.sem, self.start, self.k = sem, 0, 0

    def mark(self, ins):
        ins.then_inc(self.sem, 1)
        self.k += 1
        return self.start + self.k


def wide(ap, dim, n):
    shape = list(ap.shape)
    shape[dim] = n
    return ap.broadcast_to(shape)


def build(nc, x, up_raw, w2t, attn_raw, inv_freq, hadamard, identity, out):
    ctx = ExitStack()
    with ctx:
        def sb(name, shape, dt=FP32):
            return ctx.enter_context(nc.sbuf_tensor(name, shape, dt))

        def sem(name):
            return ctx.enter_context(nc.semaphore(name))

        up_pairs = nc.dram_tensor("up_pairs", [HT, P, 2 * 2 * KT * P], FP32).ap()
        down_pairs = nc.dram_tensor("down_pairs", [HT, P, 2 * D], FP32).ap()

        w_attn = sb("w_attn", [P, 4, 2, KT, D], FP32R)
        w_up = sb("w_up", [P, 2, 2, 2, KT, P], FP32R)
        w_down = sb("w_down", [P, 2, 2, D], FP32R)
        down_stage = w_attn[:].rearrange("p m a k n -> p (m a k n)").rearrange("p (a n) -> p a n", a=HT)
        xt = [sb(f"xt{i}", [P, 2, KT, TOK], FP32R) for i in range(2)]
        hid = sb("hid", [P, 2, 2, TOK], FP32R)
        gated = sb("gated", [P, 2, TOK])
        x_in = sb("x_in", [P, SUBS, D])
        x_mid = sb("x_mid", [P, SUBS, D])
        x_out = sb("x_out", [P, SUBS, D])
        tok = sb("tok", [P, 4 * SUBS, D])
        prod = sb("prod", [P, 3, 2 * HEADS * HD])
        scores = sb("scores", [P, 2, HEADS, HEADS])
        head_max = sb("head_max", [P, HEADS])
        head_sum = sb("head_sum", [P, HEADS])
        cos_t = sb("cos_t", [P, POS, NF])
        sin_t = sb("sin_t", [P, POS, NF])
        ident = sb("ident", [P, P])
        hada = sb("hada", [P, P])
        freq = sb("freq", [P, NF])
        stats = sb("stats", [P, SUBS, 6])
        mean_var = sb("mean_var", [P, SUBS, 2])
        rstd = sb("rstd", [P, SUBS])
        eps = sb("eps", [P, SUBS])
        mixed = sb("mixed", [P, HEADS, HD])
        carrier = sb("carrier", [P, 64])
        minus_half = sb("minus_half", [P, SUBS])

        acc = ctx.enter_context(nc.psum_tensor("acc", [P, SUBS, TOK], FP32))
        gu = ctx.enter_context(nc.psum_tensor("gu", [P, 4, TOK], FP32))

        s_ident = sem("s_ident")
        s_hada = sem("s_hada")
        s_w2 = [sem(f"s_w2_{c}") for c in range(len(W2_CUTS))]
        s_x = sem("s_x")
        s_first_x = [sem(f"s_first_x{s}") for s in range(SUBS)]
        s_attn_raw = [sem(f"s_attn_raw{m}") for m in range(4)]
        s_up_raw = [sem(f"s_up_raw{i}") for i in range(2)]
        s_up_loaded = [sem(f"s_up_loaded{i}") for i in range(2)]
        s_down_loaded = [sem(f"s_down_loaded{i}") for i in range(2)]
        s_up_stored = [sem(f"s_up_stored{i}") for i in range(2)]
        s_down_stored = [sem(f"s_down_stored{m}") for m in range(4)]
        s_freq_out = sem("s_freq_out")
        s_tabs = sem("s_tabs")
        s_trig = sem("s_trig")
        s_angle = sem("s_angle")
        s_fwht = sem("s_fwht")
        s_fwht_pool = sem("s_fwht_pool")
        s_had_ps = sem("s_had_ps")
        s_down_hi = sem("s_down_hi")
        s_down_lo = sem("s_down_lo")
        s_up_hi = sem("s_up_hi")
        s_up_lo = sem("s_up_lo")
        s_wo_hi = sem("s_wo_hi")
        s_wattn = sem("s_wattn")
        s_up_done = sem("s_up_done")
        s_silu = sem("s_silu")
        s_h = sem("s_h")
        s_hid_hi = sem("s_hid_hi")
        s_hid_lo = sem("s_hid_lo")
        s_down_done = sem("s_down_done")
        s_acc = sem("s_acc")
        s_added = sem("s_added")
        s_var = sem("s_var")
        s_eps = sem("s_eps")
        s_rstd = sem("s_rstd")
        s_ln = sem("s_ln")
        s_ln_sub = sem("s_ln_sub")
        s_xt_ps = sem("s_xt_ps")
        s_xt_hi = sem("s_xt_hi")
        s_xt_lo = sem("s_xt_lo")
        s_wo = sem("s_wo")
        s_x2 = sem("s_x2")
        s_mid = sem("s_mid")
        s_qk = sem("s_qk")
        s_rope = sem("s_rope")
        s_v_ps = sem("s_v_ps")
        s_v = sem("s_v")
        s_shift = sem("s_shift")
        s_exp = sem("s_exp")
        s_attn = sem("s_attn")
        s_shared = sem("s_shared")
        s_summed = sem("s_summed")
        s_dve = sem("s_dve")
        s_pool = sem("s_pool")

        block = ctx.enter_context(nc.Block())

        LAST = TILES - 1
        EARLY = 8

        def hidden(n, u):
            if isinstance(n, int) and n < EARLY - 4:
                return xt[1][:, 0, n, :], xt[1][:, 1, n, :]
            return hid[:, u, 0, :], hid[:, u, 1, :]

        def raw_slot(m):
            return 4 * (3 - m)

        EVEN = ((3, 3, 2), (1, 3, 2, 2, 0))
        PIECES = HEADS // 2
        SHARED = 3 * ((0, 1, 3, 4, 5, 6, 7, 9, 10, 12, 14, 15),) + ((0, 1, 3, 4, 5, 6, 7, 9, 10, 12, 13, 15),)
        POOL_BUFFERS = 3
        AHEAD = 4

        def dense_order():
            order = []
            for s in range(SUBS):
                order += [(s, u) for u in range(AHEAD if s else 0, PIECES)]
                if s + 1 < SUBS:
                    order += [(s + 1, u) for u in range(AHEAD)]
                order += [(s, PIECES + u) for u in range(PIECES)]
            at = order.index((SUBS - 1, PIECES))
            held = order.index((SUBS - 1, AHEAD)) - AHEAD
            return order[:held] + order[held + AHEAD:at] + order[held:held + AHEAD] + order[at:]

        def heads(ap):
            return ap.rearrange("p (h d) -> p h d", h=HEADS)

        def tok_at(slot):
            if isinstance(slot, int):
                return heads(tok[:, slot, :])
            return tok[:, bass.ds(slot, 1), :].rearrange("p o (h d) -> p (o h) d", h=HEADS)

        def product_buffer(b):
            if b < 3:
                return prod[:, b, :]
            return tok[:, 12 + 2 * (b - 3):14 + 2 * (b - 3), :].rearrange("p a n -> p (a n)")

        def unit_products(eng, s, u, buf, half=0):
            g = 2 * (u % PIECES)
            if u < PIECES:
                q, k = tok_at(2 * s), tok_at(2 * s + 1)
                return eng.tensor_tensor(product_buffer(buf).rearrange("p (h t d) -> p h t d", h=2, t=HEADS),
                                         wide(q[:, g:g + 2, None, :], 2, HEADS), wide(k[:, None, :, :], 1, 2), ALU.mult)
            v = tok_at(8 + s).rearrange("p t d -> p d t")
            return eng.tensor_tensor(product_buffer(buf).rearrange("p (h d t) -> p h d t", h=2, d=HD),
                                     wide(scores[:, half, g:g + 2, None, :], 2, HD), wide(v[:, None, :, :], 1, 2), ALU.mult)

        x_v = x.rearrange("(i s p) d -> i p s d", p=P, s=SUBS)
        out_v = out.rearrange("(i s p) d -> i p s d", p=P, s=SUBS)

        @block.sync
        def _(sp):
            def up_slot(u):
                return w_up[:, u].rearrange("p a b c d -> p (a b c d)").bitcast(FP32)

            def down_slot(u):
                return w_down[:, u].rearrange("p a n -> p (a n)").bitcast(FP32)

            def slab(pairs, j):
                return pairs[bass.ds(j, 1)].rearrange("o p n -> p (o n)")

            for s in range(SUBS):
                sp.dma_start(x_in[:, s, :], x_v[0][:, s, :]).then_inc(s_first_x[s], 16)
            sp.dma_start(ident[:], identity).then_inc(s_ident, 16)
            for j in range(2):
                sp.dma_start(prod[:, j, :], up_raw[j]).then_inc(s_up_raw[j], 16)
            for c in (2, 0, 1):
                sp.dma_start(tok[:, :, W2_CUTS[c]], w2t[:, :, W2_CUTS[c]].rearrange("a p n -> p a n")).then_inc(s_w2[c], 16)
            sp.dma_start(hada[:], hadamard).then_inc(s_hada, 16)
            sp.dma_start(freq[:], wide(inv_freq.rearrange("(a f) -> a f", a=1), 0, P)).then_inc(s_freq_out, 16)

            def keep_up(j, u, more):
                sp.wait_ge(s_up_hi, j + 1)
                sp.wait_ge(s_up_lo, j + 1)
                sp.dma_start(up_pairs[j], up_slot(u)).then_inc(s_up_stored[u], 16)
                if more:
                    sp.dma_start(prod[:, u, :], up_raw[j + 2]).then_inc(s_up_raw[u], 16)

            for j in range(EARLY):
                keep_up(j, j % 2, True)
            def keep_down(m):
                sp.wait_ge(s_down_hi, HT + 4 * (m + 1))
                sp.wait_ge(s_down_lo, HT + 4 * (m + 1))
                sp.dma_start(down_pairs[4 * m:4 * m + 4].rearrange("a p n -> p a n"),
                             down_stage[:, 4 * m:4 * m + 4, :].bitcast(FP32)).then_inc(s_down_stored[m], 16)

            def load_attn(m):
                if m == 0:
                    sp.wait_ge(s_down_lo, 2 * HT)
                sp.dma_start(tok[:, raw_slot(m):raw_slot(m) + 4, :], attn_raw[m]).then_inc(s_attn_raw[m], 16)

            keep_down(0)
            keep_down(1)
            for m in range(4):
                for j in range(EARLY + 2 * m, EARLY + 2 * m + 2):
                    keep_up(j, j % 2, j + 2 < HT)
                if m < 2:
                    keep_down(m + 2)
                load_attn(m)
            for u in range(2):
                sp.wait_ge(s_up_stored[u], 8 * HT)

            def load_up(j, u):
                sp.dma_start(up_slot(u), slab(up_pairs, j)).then_inc(s_up_loaded[u], 16)

            def load_down(j, u):
                sp.dma_start(down_slot(u), slab(down_pairs, j)).then_inc(s_down_loaded[u], 16)

            def weights(b):
                with sp.Fori(0, HT // 2) as jj:
                    for u in range(2):
                        sp.wait_ge(s_up_done, HT * b + 2 * jj + u - 1)
                        load_up(2 * jj + u, u)
                        sp.wait_ge(s_down_done, HT * b + 2 * jj + u - 1)
                        load_down(2 * jj + u, u)

            with sp.Fori(1, 2 * TILES) as b:
                weights(b)

        @block.tensor
        def _(pe):
            def products(o, w_hi, w_lo, m_hi, m_lo, first, last):
                nc.tensor.matmul(o, w_hi, m_hi, start=first, stop=False)
                nc.tensor.matmul(o, w_hi, m_lo, start=False, stop=False)
                return nc.tensor.matmul(o, w_lo, m_hi, start=False, stop=last)

            def xt_ready(build, k, needed=True):
                if needed:
                    pe.wait_ge(s_xt_lo, 4 * build + k + 1)

            def up(n, u, X, build=None):
                for w in range(2):
                    for k in range(KT):
                        xt_ready(build, k, build is not None and w == 0)
                        ins = products(gu[:, 2 * u + w, :], w_up[:, u, 0, w, k, :], w_up[:, u, 1, w, k, :],
                                       X[:, 0, k, :], X[:, 1, k, :], k == 0, k == KT - 1)
                ins.then_inc(s_up_done, 1)

            def down(n, u, first, last, slab=None):
                pe.wait_ge(s_hid_lo, n + 1)
                hi, lo = (w_down[:, u, 0, :], w_down[:, u, 1, :]) if slab is None else slab
                h_hi, h_lo = hidden(n, u)
                for s in range(SUBS):
                    ins = products(acc[:, s, :], h_hi[:, s * P:(s + 1) * P], h_lo[:, s * P:(s + 1) * P], hi, lo, first, last)
                    if last and s < SUBS - 1:
                        ins.then_inc(s_acc, 1)
                ins.then_inc(s_down_done, 1)

            def staged(j):
                if isinstance(j, int):
                    return down_stage[:, j, 0:D], down_stage[:, j, D:2 * D]
                flat = down_stage.rearrange("p a n -> p (a n)")
                return flat[:, bass.ds(j * 2 * D, D)], flat[:, bass.ds(j * 2 * D + D, D)]

            def transposes(src, bank, ks):
                for k in ks:
                    for s in range(SUBS):
                        ins = nc.tensor.transpose(bank[:, k, s * P:(s + 1) * P], tok[:, src(s), k * P:(k + 1) * P], ident[:])
                    ins.then_inc(s_xt_ps, 1)

            def transposes_by_sub(src, bank, sub_ready):
                for s in range(SUBS):
                    sub_ready(s)
                    for k in range(KT):
                        ins = nc.tensor.transpose(bank[:, k, s * P:(s + 1) * P], src(s, k), ident[:])
                        if s == SUBS - 1:
                            ins.then_inc(s_xt_ps, 1)

            def sub_normed(l):
                return lambda s: pe.wait_ge(s_ln, l + 1) if s == SUBS - 1 else pe.wait_ge(s_ln_sub, (SUBS - 1) * l + s + 1)

            def normed(s, k):
                return tok[:, 12 + s, k * P:(k + 1) * P]

            def ffn(b, X, x_build, before_build=None, src=None, dense=None, values=None):
                n0 = HT * b

                def up_step(jj, u, x_build=None):
                    pe.wait_ge(s_up_loaded[u], 16 * (HT // 2 * (b - 1) + jj + 1))
                    up(n0 + 2 * jj + u, u, X, x_build)

                def down_step(jj, u, first, last):
                    pe.wait_ge(s_down_loaded[u], 16 * (HT // 2 * (b - 1) + jj + 1))
                    down(n0 + 2 * jj + u, u, first, last)

                if values is not None:
                    pe.wait_ge(s_v, values - 2)
                up_step(0, 0, x_build)
                if values is not None:
                    pe.wait_ge(s_v, values)
                up_step(0, 1)
                pe.wait_ge(s_added, SUBS * b)
                down_step(0, 0, True, False)
                with pe.Fori(1, HT // 2) as jj:
                    for u in range(2):
                        pe.wait_ge(s_h, n0 + 2 * jj + u - 1)
                        up_step(jj, u)
                        down_step(jj - 1 + u, 1 - u, False, False)
                if dense is not None:
                    down_step(HT // 2 - 1, 1, False, True)
                    pe.wait_ge(s_h, n0 + HT)
                    transposes_by_sub(lambda s, k: tok[:, 2 * s, k * P:(k + 1) * P], gu,
                                      lambda s: pe.wait_ge(s_attn, dense + s + 1))
                    return
                if before_build is not None:
                    before_build()
                    pe.wait_ge(s_h, n0 + HT - 1)
                    transposes(src, gu, (0, 1))
                    pe.wait_ge(s_h, n0 + HT)
                    transposes(src, gu, (2, 3))
                down_step(HT // 2 - 1, 1, False, True)

            def block_0(X):
                def up_step(n, u, wait=True):
                    pe.wait_ge(s_up_hi, n + 1)
                    pe.wait_ge(s_up_lo, n + 1)
                    if wait:
                        pe.wait_ge(s_h, n - 1)
                    up(n, u, X)

                for n in range(EARLY):
                    up_step(n, n % 2, n >= 2)
                hadamard_products()
                pe.wait_ge(s_down_lo, 2 * HT)
                pe.wait_ge(s_down_hi, 2 * HT)
                for n in range(EARLY - 1):
                    down(n, n % 2, n == 0, False, staged(n))
                with pe.Fori(EARLY // 2, HT // 2) as jj:
                    for u in range(2):
                        n = 2 * jj + u
                        up_step(n, u)
                        down(n - 1, 1 - u, False, False, staged(n - 1))
                down(HT - 1, 1, False, True, staged(HT - 1))

            def project(m, o, X, s, build=None):
                for k in range(KT):
                    xt_ready(build, k, build is not None)
                    ins = products(o, X[:, 0, k, s * P:(s + 1) * P], X[:, 1, k, s * P:(s + 1) * P],
                                   w_attn[:, m, 0, k, :], w_attn[:, m, 1, k, :], k == 0, k == KT - 1)
                return ins

            def qkv(i, X, ln, build, first):
                for s in range(SUBS):
                    if s < 2:
                        if not first:
                            pe.wait_ge(s_x2, SUBS * (i - 1) + 2 * s + 2)
                    else:
                        pe.wait_ge(s_rope, SUBS * i + s - 1)
                    for m in (Q, K):
                        ins = project(m, gu[:, 2 * (s % 2) + m, :], X, s, build if (s, m) == (0, Q) else None)
                    ins.then_inc(s_qk, 1)
                    if s == 1 and not first:
                        pe.wait_ge(s_ln, ln + 1)
                        transposes(lambda t: 12 + t, acc, range(KT))
                for s in range(SUBS):
                    pe.wait_ge(s_rope, SUBS * i + s // 2 + 3)
                    project(V, gu[:, s, :], X, s).then_inc(s_v_ps, 1)

            def hadamard_products():
                pe.wait_ge(s_hada, 16)
                for part, transformed in enumerate((s_fwht, s_fwht_pool)):
                    pe.wait_ge(transformed, 1)
                    for a in range(HT):
                        n = HT * part + a
                        if n >= 4:
                            pe.wait_ge(s_down_hi, n - 3)
                            pe.wait_ge(s_down_lo, n - 3)
                        nc.tensor.matmul(acc[:, a % 4, PARTS[part]], hada[:], tok[:, a, PARTS[part]],
                                         start=True, stop=True).then_inc(s_had_ps, 1)

            pe.wait_ge(s_ident, 16)
            transposes_by_sub(lambda s, k: x_mid[:, s, k * P:(k + 1) * P], gu, sub_normed(0))
            pe.wait_ge(s_xt_lo, 4)
            block_0(xt[0])
            pe.wait_ge(s_added, SUBS)
            transposes_by_sub(normed, acc, sub_normed(1))
            pe.wait_ge(s_wattn, 3)
            qkv(0, xt[0], None, 1, True)
            pe.wait_ge(s_ln, 3)
            pe.wait_ge(s_v, SUBS)
            transposes(lambda s: 12 + s, gu, range(KT))

            def wo(i, build):
                for s in range(SUBS):
                    if s < 2:
                        xt_ready(build, 2 * s + 1)
                    project(O, gu[:, s, :], xt[1], s, build if s == 0 else None).then_inc(s_wo, 1)

            def iteration(i, first, last):
                e, l = 3 + 4 * (i - 1), 3 + 3 * (i - 1)
                if first:
                    ffn(1, xt[0], e - 1, dense=0)
                else:
                    ffn(2 * i - 1, xt[0], e - 1, lambda: pe.wait_ge(s_attn, SUBS * i), lambda s: 2 * s)
                wo(i, e)
                pe.wait_ge(s_ln, l + 1)
                transposes(lambda s: 12 + s, acc, range(KT))
                qkv(i, xt[0], l + 1, e + 1, False)
                v = SUBS * (i + 1)
                if last:
                    ffn(2 * i, xt[1], e + 2, dense=SUBS * i, values=v)
                else:
                    ffn(2 * i, xt[1], e + 2, lambda: pe.wait_ge(s_ln, l + 3), lambda s: 12 + s, values=v)

            iteration(1, True, False)
            with pe.Fori(2, LAST) as i:
                iteration(i, False, False)
            iteration(LAST, False, True)
            e, l = 3 + 4 * LAST - 1, 3 + 3 * LAST - 1
            wo(TILES, e)
            pe.wait_ge(s_added, SUBS * (2 * TILES - 1))
            transposes_by_sub(normed, acc, sub_normed(l))
            pe.wait_ge(s_x2, SUBS * TILES)
            ffn(2 * TILES - 1, xt[1], e + 1)

        @block.scalar
        def _(act):
            def silu(n, u, wait):
                act.wait_ge(s_up_done, n + 1)
                if wait:
                    act.wait_ge(s_hid_lo, n - 1)
                nc.scalar.activation(gated[:, u, :], gu[:, 2 * u, :], ACT.Silu).then_inc(s_silu, 1)

            def hid_high(n, u, wait):
                act.wait_ge(s_h, n + 1)
                if wait:
                    act.wait_ge(s_down_done, n - 1)
                nc.scalar.activation(hidden(n, u)[0], gated[:, u, :], ACT.Copy).then_inc(s_hid_hi, 1)

            def xt_high(X, bank, build):
                for k in range(KT):
                    act.wait_ge(s_xt_ps, 4 * build + k + 1)
                    nc.scalar.activation(X[:, 0, k, :], bank[:, k, :], ACT.Copy).then_inc(s_xt_hi, 1)

            def ffn(b, attention, dense=False):
                n0 = HT * b
                if attention is None:
                    with act.Fori(0, HT // 2) as jj:
                        for u in range(2):
                            silu(n0 + 2 * jj + u, u, True)
                            hid_high(n0 + 2 * jj + u, u, True)
                elif dense:
                    per = HT // SUBS
                    for n in range(HT):
                        silu(n0 + n, n % 2, True)
                        hid_high(n0 + n, n % 2, True)
                        s = n // per
                        if n == s * per + (2 if s < SUBS - 1 else 1):
                            exp(attention + s, s % 2)
                else:
                    steps = len(EVEN[0]) + len(EVEN[1])
                    with act.Fori(0, HT // steps) as h:
                        for j in range(steps):
                            silu(n0 + steps * h + j, j % 2, True)
                            hid_high(n0 + steps * h + j, j % 2, True)
                            if j == len(EVEN[0]):
                                exp(attention + h)

            def exp(c, half=0):
                act.wait_ge(s_shift, c + 1)
                nc.scalar.activation(scores[:, half], scores[:, half], ACT.Exp, scale=SCORE_SCALE).then_inc(s_exp, 1)

            def up_high(n, jj, u, wait):
                act.wait_ge(s_up_raw[u], 16 * (jj + 1))
                if wait:
                    act.wait_ge(s_up_done, n - 1)
                    act.wait_ge(s_up_stored[u], 16 * jj)
                nc.scalar.activation(w_up[:, u, 0].rearrange("p a b c -> p (a b c)"), prod[:, u, :], ACT.Copy).then_inc(s_up_hi, 1)

            def ffn_step(n, u, wait):
                silu(n, u, wait)
                hid_high(n, u, wait)

            up_high(0, 0, 0, False)
            up_high(1, 0, 1, False)
            xt_high(xt[0], gu, 0)
            for n in range(EARLY - 2):
                silu(n, n % 2, n >= 2)
                hid_high(n, n % 2, False)
                up_high(n + 2, n // 2 + 1, n % 2, True)
            for u in range(2):
                silu(EARLY - 2 + u, u, True)
            for part, cols in enumerate(PARTS):
                for a in range(HT):
                    act.wait_ge(s_had_ps, HT * part + a + 1)
                    nc.scalar.activation(down_stage[:, a, cols], acc[:, a % 4, cols], ACT.Copy, scale=DOWN_SCALE)\
                        .then_inc(s_down_hi, 1)
            for u in range(2):
                hid_high(EARLY - 2 + u, u, True)
                up_high(EARLY + u, EARLY // 2, u, True)
            act.wait_ge(s_angle, 1)
            nc.scalar.activation(sin_t[:, 0:POS], sin_t[:, 0:POS], ACT.Sin).then_inc(s_trig, 1)
            nc.scalar.activation(cos_t[:, 0:POS], cos_t[:, 0:POS], ACT.Sin).then_inc(s_trig, 1)
            with act.Fori(EARLY // 2, HT // 2 - 1) as jj:
                for u in range(2):
                    ffn_step(2 * jj + u, u, True)
                    up_high(2 * jj + u + 2, jj + 1, u, True)
            for u in range(2):
                ffn_step(HT - 2 + u, u, True)
            act.wait_ge(s_attn_raw[O], 16)
            act.wait_ge(s_down_stored[O], 16)
            act.wait_ge(s_down_done, HT)
            nc.scalar.activation(w_attn[:, O, 0], tok[:, raw_slot(O):raw_slot(O) + 4, :], ACT.Copy).then_inc(s_wo_hi, 1)

            def move_x(i):
                act.wait_ge(s_added, SUBS * (2 * i) if not isinstance(i, int) or i > 0 else SUBS)
                act.wait_ge(s_ln, 3 + 3 * (i - 1) + 1 if not isinstance(i, int) or i > 0 else 2)
                if not isinstance(i, int) or i > 0:
                    act.wait_ge(s_x2, SUBS * i)
                nc.scalar.activation(x_mid[:], x_in[:], ACT.Copy).then_inc(s_mid, 1)

            def load_x(i):
                act.wait_ge(s_mid, i)
                act.dma_start(x_in[:], x_v[i] if isinstance(i, int) else
                              x_v[bass.ds(i, 1)].rearrange("o p s d -> p (o s) d")).then_inc(s_x, 16)

            def store_out(i):
                act.wait_ge(s_added, SUBS * (2 * i + 3))
                act.dma_start(out_v[i] if isinstance(i, int) else
                              out_v[bass.ds(i, 1)].rearrange("o p s d -> p (o s) d"), x_out[:]).then_inc(s_freq_out, 16)

            def values(i):
                for s in range(SUBS):
                    act.wait_ge(s_v_ps, SUBS * i + s + 1)
                    nc.scalar.activation(tok[:, 8 + s, :], gu[:, s, :], ACT.Copy).then_inc(s_v, 1)

            xt_high(xt[0], acc, 1)
            move_x(0)
            load_x(1)
            values(0)
            xt_high(xt[0], gu, 2)

            def iteration(i, first, last):
                e = 3 + 4 * (i - 1)
                if first:
                    ffn(1, 0, True)
                else:
                    ffn(2 * i - 1, SUBS * (i - 1) + 2)
                xt_high(xt[1], gu, e)
                xt_high(xt[0], acc, e + 1)
                move_x(i)
                if not last:
                    load_x(i + 1)
                xt_high(xt[1], acc, e + 2)
                values(i)
                if last:
                    ffn(2 * i, SUBS * i, True)
                    xt_high(xt[1], gu, e + 3)
                else:
                    ffn(2 * i, SUBS * i)
                    xt_high(xt[0], gu, e + 3)
                store_out(i - 1)

            iteration(1, True, False)
            with act.Fori(2, LAST) as i:
                iteration(i, False, False)
            iteration(LAST, False, True)
            xt_high(xt[1], acc, 3 + 4 * LAST)
            ffn(2 * TILES - 1, None)
            for s in range(SUBS):
                act.wait_ge(s_added, SUBS * (2 * TILES - 1) + s + 1)
                act.dma_start(out_v[LAST][:, s, :], x_out[:, s, :]).then_inc(s_freq_out, 16)
            act.wait_ge(s_freq_out, 16 * (TILES + SUBS))

        @block.gpsimd
        def _(pool):
            nc.gpsimd.memset(minus_half[:], -0.5).then_inc(s_tabs, 1)
            nc.gpsimd.memset(eps[:], EPS).then_inc(s_tabs, 1)
            nc.gpsimd.iota(scores[:, 0].rearrange("p a b -> p (a b)")[:, 0:POS], pattern=[[P, POS]], base=0,
                           channel_multiplier=1, allow_small_or_imprecise_dtypes=True).then_inc(s_tabs, 1)
            pool.wait_ge(s_tabs, 3)

            def inverse_root(l):
                pool.wait_ge(s_var, l + 1)
                nc.gpsimd.tensor_tensor(rstd[:], mean_var[:, :, 1], eps[:], ALU.add).then_inc(s_eps, 1)
                pool.wait_ge(s_eps, l + 1)
                nc.gpsimd.tensor_tensor(rstd[:], rstd[:], minus_half[:], ALU.pow).then_inc(s_rstd, 1)

            inverse_root(0)
            width = W2_CUTS[-1].stop - W2_CUTS[-1].start
            pool.wait_ge(s_w2[-1], 16)
            sums = x_out[:].rearrange("p s n -> p (s n)")[:, 0:HT // 2 * width].rearrange("p (t n) -> p t n", n=width)
            steps = 0
            for st in (1, 2, 4, 8):
                v = tok[:, :, W2_CUTS[-1]].rearrange("p (g e t) n -> p g e t n", e=2, t=st)
                a, b = v[:, :, 0], v[:, :, 1]
                both = sums.rearrange("p (g t) n -> p g t n", t=st)
                nc.gpsimd.tensor_tensor(both, a, b, ALU.add).then_inc(s_pool, 1)
                nc.gpsimd.tensor_tensor(b, a, b, ALU.subtract).then_inc(s_pool, 1)
                pool.wait_ge(s_pool, steps + 2)
                nc.gpsimd.tensor_copy(a, both).then_inc(s_pool, 1)
                steps += 3
                pool.wait_ge(s_pool, steps)
            nc.gpsimd.memset(eps[:], EPS).then_inc(s_fwht_pool, 1)
            for m in range(4):
                if m == O:
                    inverse_root(1)
                pool.wait_ge(s_attn_raw[m], 16)
                pool.wait_ge(s_down_stored[m], 16)
                pool.wait_ge(s_down_done, 4 * (m + 1))
                raw = tok[:, raw_slot(m):raw_slot(m) + 4, :]
                if m == O:
                    pool.wait_ge(s_wo_hi, 1)
                else:
                    nc.gpsimd.tensor_copy(w_attn[:, m, 0], raw).then_inc(s_pool, 1)
                    pool.wait_ge(s_pool, steps + m + 1)
                nc.gpsimd.tensor_tensor(w_attn[:, m, 1], raw, w_attn[:, m, 0].bitcast(FP32), ALU.subtract).then_inc(s_wattn, 1)

            def shared_products(i, k, last_build):
                pool.wait_ge(s_xt_ps, 4 * (last_build + 1))
                for s, u in dense_order():
                    if u in SHARED[s]:
                        if u < PIECES:
                            pool.wait_ge(s_rope, SUBS * i + s + 1)
                        else:
                            pool.wait_ge(s_exp, SUBS * i + s + 1)
                        if k >= POOL_BUFFERS:
                            pool.wait_ge(s_summed, k - POOL_BUFFERS + 1)
                        unit_products(nc.gpsimd, s, u, 2 + k % POOL_BUFFERS, s % 2).then_inc(s_shared, 1)
                        k += 1
                return k

            inverse_root(2)
            shared = shared_products(0, 0, 2)
            with pool.Fori(3, 2 + 3 * LAST) as l:
                inverse_root(l)
            shared_products(LAST, shared, 3 + 4 * (LAST - 1) + 2)
            inverse_root(2 + 3 * LAST)

        @block.vector
        def _(dve):
            chain = Count(s_dve)

            def link(ins):
                dve.wait_ge(s_dve, chain.mark(ins))

            places = iter(range(1, 64))

            def small_copy():
                at = next(places)
                return nc.vector.tensor_copy(carrier[:, at:at + 1], carrier[:, 0:1])

            def carry(sem, value):
                dve.wait_ge(sem, value)
                small_copy()

            def h_and_low(n, u, between):
                dve.wait_ge(s_silu, n + 1)
                nc.vector.tensor_tensor(gated[:, u, :], gated[:, u, :], gu[:, 2 * u + 1, :], ALU.mult).then_inc(s_h, 1)
                between()
                dve.wait_ge(s_hid_hi, n + 1)
                high, low = hidden(n, u)
                nc.vector.tensor_tensor(low, gated[:, u, :], high.bitcast(FP32), ALU.subtract)\
                    .then_inc(s_hid_lo, 1)

            def xt_low(X, bank, build):
                for k in range(KT):
                    dve.wait_ge(s_xt_hi, 4 * build + k + 1)
                    nc.vector.tensor_tensor(X[:, 1, k, :], bank[:, k, :], X[:, 0, k, :].bitcast(FP32), ALU.subtract)\
                        .then_inc(s_xt_lo, 1)

            def l_is_later(l):
                return not isinstance(l, int) or l > 0

            def layer_norm(src, dst, l, add=lambda s: None, added=lambda s: None):
                add(0)
                for s in range(SUBS):
                    if s + 1 < SUBS:
                        add(s + 1)
                    added(s)
                    at = chain.mark(nc.vector.bn_stats(stats[:, s, :], src[:, s, :]))
                carry(s_dve, at)
                if l_is_later(l):
                    carry(s_ln, l)
                for s in range(SUBS):
                    ins = nc.vector.bn_aggr(mean_var[:, s, :], stats[:, s, :])
                ins.then_inc(s_var, 1)
                dve.wait_ge(s_rstd, l + 1)
                for s in range(SUBS):
                    nc.vector.tensor_scalar(dst(s), src[:, s, :], mean_var[:, s, 0:1], rstd[:, s:s + 1],
                                            ALU.subtract, ALU.mult).then_inc(s_ln_sub if s < SUBS - 1 else s_ln, 1)

            def add_sum(b, x, s):
                if s < SUBS - 1:
                    dve.wait_ge(s_acc, (SUBS - 1) * b + s + 1)
                else:
                    dve.wait_ge(s_down_done, HT * (b + 1))
                nc.vector.tensor_tensor(x[:, s, :], x[:, s, :], acc[:, s, :], ALU.add).then_inc(s_added, 1)

            def add_sums(b, x):
                for s in range(SUBS):
                    add_sum(b, x, s)

            def norm_of_sums(b, l):
                layer_norm(x_in, normed, l, lambda s: add_sum(b, x_in, s), lambda s: dve.wait_ge(s_added, SUBS * b + s + 1))

            def unit_sum(u, buf, half=0):
                g = 2 * (u % PIECES)
                if u < PIECES:
                    return nc.vector.tensor_reduce(scores[:, half, g:g + 2, :],
                                                   product_buffer(buf).rearrange("p (h t d) -> p h t d", h=2, t=HEADS), AX.X, ALU.add)
                return nc.vector.tensor_reduce(mixed[:, g:g + 2, :],
                                               product_buffer(buf).rearrange("p (h d t) -> p h d t", h=2, d=HD), AX.X, ALU.add)

            def shift(last_sum, half=0):
                dve.wait_ge(*last_sum)
                link(nc.vector.tensor_reduce(head_max[:], scores[:, half], AX.X, ALU.max))
                nc.vector.tensor_tensor(scores[:, half], scores[:, half], wide(head_max[:, :, None], 2, HEADS), ALU.subtract)\
                    .then_inc(s_shift, 1)

            def row_sums(c, half=0):
                dve.wait_ge(s_exp, c + 1)
                dve.wait_ge(s_attn, c)
                link(nc.vector.tensor_reduce(head_sum[:], scores[:, half], AX.X, ALU.add))
                chain.mark(nc.vector.reciprocal(head_sum[:], head_sum[:]))

            def divide(last_sum, s):
                dve.wait_ge(*last_sum)
                nc.vector.tensor_tensor(tok_at(2 * s), mixed[:], wide(head_sum[:, :, None], 2, HD), ALU.mult).then_inc(s_attn, 1)

            CHAIN_SUB = 4 * PIECES + 3

            def attention_sub(s, c, step):
                free = [chain.start + chain.k] * 2
                made = []
                units = iter(range(2 * PIECES))
                buffers = itertools.cycle((0, 1))

                def products_of(u):
                    buf = next(buffers)
                    dve.wait_ge(s_dve, free[buf])
                    made.append((u, buf, chain.mark(unit_products(nc.vector, s, u, buf))))

                def sum_of_oldest():
                    u, buf, at = made.pop(0)
                    dve.wait_ge(s_dve, at)
                    free[buf] = chain.mark(unit_sum(u, buf))
                    return s_dve, free[buf]

                for j, n in enumerate(EVEN[0] + EVEN[1]):
                    scored = j == len(EVEN[0])
                    mine = [next(units) for _ in range(n)]
                    if j == len(EVEN[0] + EVEN[1]) - 1:
                        divide(done, s)
                    if scored:
                        step(j, lambda: None)
                        row_sums(c)
                    else:
                        step(j, lambda: products_of(mine.pop(0)) if mine else None)
                    if mine and (made or scored):
                        products_of(mine.pop(0))
                    while made:
                        done = sum_of_oldest()
                        if mine:
                            products_of(mine.pop(0))
                    if j == len(EVEN[0]) - 1:
                        shift(done)
                assert n == 0 and next(units, None) is None

            pooled = itertools.count()

            def attention_dense(c, step):
                free = [chain.start + chain.k] * 2
                products = {}
                buffers = itertools.cycle((0, 1))
                per = HT // SUBS
                order = dense_order()

                def make(s, u):
                    buf = next(buffers)
                    dve.wait_ge(s_dve, free[buf])
                    products[s, u] = buf, chain.mark(unit_products(nc.vector, s, u, buf, s % 2))

                def unit(s, u, following=None):
                    if u == PIECES:
                        row_sums(c + s, s % 2)
                    if u in SHARED[s]:
                        n = next(pooled)
                        dve.wait_ge(s_shared, n + 1)
                        unit_sum(u, 2 + n % POOL_BUFFERS, s % 2).then_inc(s_summed, 1)
                        done = s_summed, n + 1
                    else:
                        if (s, u) not in products:
                            make(s, u)
                        if following is not None and following[1] not in SHARED[following[0]] + (PIECES,):
                            make(*following)
                        buf, at = products.pop((s, u))
                        dve.wait_ge(s_dve, at)
                        free[buf] = chain.mark(unit_sum(u, buf, s % 2))
                        done = s_dve, free[buf]
                    if u == PIECES - 1:
                        shift(done, s % 2)
                    if u == 2 * PIECES - 1:
                        divide(done, s)

                for n in range(HT):
                    mine = order[per * n:per * n + per]
                    step(n, lambda: unit(*mine[0], mine[1]))
                    for at in range(1, per):
                        unit(*mine[at], mine[at + 1] if at + 1 < per else None)

            def ffn(b, first_sub, c, dense=False):
                n0 = HT * b
                if first_sub is None:
                    with dve.Fori(0, HT // 2) as jj:
                        for u in range(2):
                            h_and_low(n0 + 2 * jj + u, u, lambda: None)
                    return
                if dense:
                    attention_dense(c, lambda n, between: h_and_low(n0 + n, n % 2, between))
                    return
                steps = len(EVEN[0]) + len(EVEN[1])
                start = chain.start + chain.k
                with dve.Fori(0, HT // steps) as h:
                    chain.start, chain.k = start + CHAIN_SUB * h, 0
                    attention_sub(h + first_sub, c + h, lambda j, between: h_and_low(n0 + steps * h + j, j % 2, between))
                    assert chain.k == CHAIN_SUB, chain.k
                chain.start, chain.k = start + HT // steps * CHAIN_SUB, 0

            def rope(i, s):
                dve.wait_ge(s_qk, SUBS * i + s + 1)
                src = gu[:, 2 * (s % 2):2 * (s % 2) + 2, :].rearrange("p m (h f e) -> p (m h) f e", h=HEADS, e=2)
                x1, x2 = src[:, :, :, 0], src[:, :, :, 1]
                dst = tok[:, 2 * s:2 * s + 2, :].rearrange("p m (h e f) -> p (m h) e f", h=HEADS, e=2)

                def table(t):
                    at = (SUBS * i + s) % POS
                    a = t[:, at:at + 1, :] if isinstance(i, int) else t[:, bass.ds(at, 1), :]
                    return wide(a, 1, 2 * HEADS)

                def tmp(r, part):
                    return prod[:, r, :].rearrange("p (e h f) -> p e h f", e=2, h=2 * HEADS)[:, part]

                dve.wait_ge(s_dve, chain.start + chain.k)
                at = []
                for r, part, a, t in ((0, 0, x1, cos_t), (0, 1, x2, sin_t), (1, 0, x1, sin_t), (1, 1, x2, cos_t)):
                    ins = nc.vector.tensor_tensor(tmp(r, part), a, table(t), ALU.mult)
                    at.append(chain.mark(ins))
                dve.wait_ge(s_dve, at[1])
                nc.vector.tensor_tensor(dst[:, :, 0, :], tmp(0, 0), tmp(0, 1), ALU.subtract)
                dve.wait_ge(s_dve, at[3])
                link(nc.vector.tensor_tensor(dst[:, :, 1, :], tmp(1, 0), tmp(1, 1), ALU.add))
                small_copy().then_inc(s_rope, 1)

            def up_low(n, u):
                dve.wait_ge(s_up_hi, n + 1)
                nc.vector.tensor_tensor(w_up[:, u, 1].rearrange("p a b c -> p (a b c)"), prod[:, u, :],
                                        w_up[:, u, 0].rearrange("p a b c -> p (a b c)").bitcast(FP32), ALU.subtract).then_inc(s_up_lo, 1)

            link(nc.vector.memset(carrier[:, 0:1], 0.0))
            layer_norm(x_in, lambda s: x_mid[:, s, :], 0, added=lambda s: dve.wait_ge(s_first_x[s], 16))
            up_low(0, 0)
            xt_low(xt[0], gu, 0)
            up_low(1, 1)
            def hidden_step(n):
                h_and_low(n, n % 2, lambda: None)

            for c in range(2):
                dve.wait_ge(s_w2[c], 16)
                for level, st in enumerate((1, 2, 4, 8)):
                    v = tok[:, :, W2_CUTS[c]].rearrange("p (g e t) n -> p g e t n", e=2, t=st)
                    a, b = v[:, :, 0], v[:, :, 1]
                    link(nc.vector.tensor_tensor(b, a, b, ALU.subtract))
                    if st == 1:
                        pairs = [(a[:, :, 0], b[:, :, 0])]
                    else:
                        pairs = [(a[:, g], b[:, g]) for g in range(HT // (2 * st))]
                    for pa, pb in pairs:
                        at = chain.mark(nc.vector.scalar_tensor_tensor(pa, pa, 2.0, pb, ALU.mult, ALU.subtract))
                    done = 4 * c + level + 1
                    if done == 2:
                        hidden_step(0)
                    if done in (3, 4):
                        up_low(done - 1, (done - 1) % 2)
                    if done == 3:
                        hidden_step(1)
                    if done in (5, 6, 7):
                        hidden_step(done - 3)
                        up_low(done - 1, (done - 1) % 2)
                    dve.wait_ge(s_dve, at)
            small_copy().then_inc(s_fwht, 1)
            hidden_step(EARLY - 3)
            up_low(EARLY - 1, 1)
            for part, cols in enumerate(PARTS):
                for a in range(HT):
                    dve.wait_ge(s_down_hi, HT * part + a + 1)
                    nc.vector.scalar_tensor_tensor(down_stage[:, a, D + cols.start:D + cols.stop], acc[:, a % 4, cols], DOWN_SCALE,
                                                   down_stage[:, a, cols].bitcast(FP32), ALU.mult, ALU.subtract).then_inc(s_down_lo, 1)
            for u in range(2):
                hidden_step(EARLY - 2 + u)
                up_low(EARLY + u, u)
            dve.wait_ge(s_freq_out, 16)
            dve.wait_ge(s_tabs, 3)
            pos = scores[:, 0].rearrange("p a b -> p (a b)")[:, 0:POS]
            spare = mixed[:].rearrange("p a b -> p (a b)")
            angle = spare[:, 0:POS * NF].rearrange("p (a b) -> p a b", a=POS)
            turns = spare[:, POS * NF:2 * POS * NF].rearrange("p (a b) -> p a b", a=POS)
            link(nc.vector.tensor_tensor(angle, wide(pos[:, :, None], 2, NF), wide(freq[:, None, :], 1, POS), ALU.mult))
            MAGIC = 1.5 * 2.0 ** 23
            TWO_PI = 2.0 * np.pi
            C1 = 6.28125
            C2 = float(np.float32(np.round((TWO_PI - C1) * 2.0 ** 21) / 2.0 ** 21))
            C3 = float(np.float32(TWO_PI - C1 - C2))
            LIMIT = float(np.float32(3.1415925))
            for table, quarter in ((sin_t, 0.0), (cos_t, 0.25)):
                r = table[:, 0:POS]
                link(nc.vector.tensor_scalar(turns, angle, float(1.0 / TWO_PI), quarter, ALU.mult, ALU.add))
                link(nc.vector.tensor_scalar(turns, turns, MAGIC, None, ALU.add))
                link(nc.vector.tensor_scalar(turns, turns, MAGIC, None, ALU.subtract))
                link(nc.vector.scalar_tensor_tensor(r, turns, -C1, angle, ALU.mult, ALU.add))
                link(nc.vector.scalar_tensor_tensor(r, turns, -C2, r, ALU.mult, ALU.add))
                link(nc.vector.scalar_tensor_tensor(r, turns, -C3, r, ALU.mult, ALU.add))
                if quarter:
                    link(nc.vector.tensor_scalar(r, r, float(np.pi / 2), None, ALU.add))
                link(nc.vector.tensor_scalar(r, r, LIMIT, -LIMIT, ALU.min, ALU.max))
            small_copy().then_inc(s_angle, 1)
            with dve.Fori(EARLY // 2, HT // 2 - 1) as jj:
                for u in range(2):
                    h_and_low(2 * jj + u, u, lambda: None)
                    up_low(2 * jj + u + 2, u)
            for u in range(2):
                h_and_low(HT - 2 + u, u, lambda: None)

            def normed(s):
                return tok[:, 12 + s, :]

            dve.wait_ge(s_wattn, 1)
            norm_of_sums(0, 1)
            xt_low(xt[0], acc, 1)
            dve.wait_ge(s_trig, 2)
            dve.wait_ge(s_wattn, 4)
            for s in range(SUBS):
                rope(0, s)
            dve.wait_ge(s_x, 16)
            layer_norm(x_in, normed, 2)
            xt_low(xt[0], gu, 2)
            carry(s_v, SUBS)

            def add_attention(i, s):
                if s == 0:
                    dve.wait_ge(s_freq_out, 16 * i)
                    dve.wait_ge(s_mid, i)
                dve.wait_ge(s_wo, SUBS * (i - 1) + s + 1)
                nc.vector.tensor_tensor(x_out[:, s, :], x_mid[:, s, :], gu[:, s, :], ALU.add).then_inc(s_x2, 1)

            def iteration(i, first, last):
                e, l = 3 + 4 * (i - 1), 3 + 3 * (i - 1)
                if first:
                    ffn(1, 0, 0, True)
                else:
                    ffn(2 * i - 1, 2, SUBS * (i - 1) + 2)
                xt_low(xt[1], gu, e)
                norm_of_sums(2 * i - 1, l)
                for s in range(SUBS):
                    add_attention(i, s)
                xt_low(xt[0], acc, e + 1)
                dve.wait_ge(s_x2, SUBS * i)
                layer_norm(x_out, normed, l + 1)
                rope(i, 0)
                rope(i, 1)
                xt_low(xt[1], acc, e + 2)
                rope(i, 2)
                rope(i, 3)
                if not last:
                    dve.wait_ge(s_x, 16 * (i + 1))
                    layer_norm(x_in, normed, l + 2)
                carry(s_v, SUBS * (i + 1))
                if last:
                    ffn(2 * i, 0, SUBS * i, True)
                    xt_low(xt[1], gu, e + 3)
                else:
                    ffn(2 * i, 0, SUBS * i)
                    xt_low(xt[0], gu, e + 3)
                add_sums(2 * i, x_out)

            iteration(1, True, False)
            start = chain.start + chain.k
            PER = 3 * SUBS + 4 * CHAIN_SUB + 5 * SUBS
            with dve.Fori(2, LAST) as i:
                chain.start, chain.k = start + PER * (i - 2), 0
                iteration(i, False, False)
            chain.start, chain.k = start + PER * (LAST - 2), 0
            iteration(LAST, False, True)
            layer_norm(x_out, normed, 3 + 3 * LAST - 1, lambda s: add_attention(TILES, s),
                       lambda s: dve.wait_ge(s_x2, SUBS * LAST + s + 1))
            xt_low(xt[1], acc, 3 + 4 * LAST)
            ffn(2 * TILES - 1, None, None)
            add_sums(2 * TILES - 1, x_out)


def hadamard_128():
    h = np.ones((1, 1), np.float32)
    while h.shape[0] < P:
        h = np.block([[h, h], [h, -h]]).astype(np.float32)
    return h


def kernel(L0_attn_x, L0_attn_wq, L0_attn_wk, L0_attn_wv, L0_attn_wo, L0_attn_inv_freq, L0_ffn_W1, L0_ffn_W2, L0_ffn_W3):
    import concourse.bacc as bacc
    from concourse.bass_utils import run_bass_kernel_spmd

    def contraction_major(w, n):
        return np.asarray(w).reshape(-1, n, KT, P).transpose(0, 3, 2, 1)

    w1, w3 = contraction_major(L0_ffn_W1, P), contraction_major(L0_ffn_W3, P)
    arrays = {
        "x": np.asarray(L0_attn_x).reshape(B * S, D),
        "up_raw": np.stack([w1, w3], axis=2).reshape(HT, P, 2 * KT * P),
        "w2t": np.asarray(L0_ffn_W2).T.reshape(HT, P, D),
        "attn_raw": np.stack([contraction_major(w, D)[0] for w in (L0_attn_wq, L0_attn_wk, L0_attn_wv, L0_attn_wo)]),
        "inv_freq": np.asarray(L0_attn_inv_freq),
        "hadamard": hadamard_128(),
        "identity": np.eye(P, dtype=np.float32),
    }
    arrays = {name: np.ascontiguousarray(a) for name, a in arrays.items()}
    nc = bacc.Bacc("TRN2", target_bir_lowering=False, num_devices=1)
    aps = [nc.dram_tensor(name, a.shape, FP32, kind="ExternalInput").ap() for name, a in arrays.items()]
    out = nc.dram_tensor("out", (B * S, D), FP32, kind="ExternalOutput").ap()
    build(nc, *aps, out)
    r = run_bass_kernel_spmd(nc, [arrays], core_ids=[0])
    return r.results[0]["out"].reshape(B, S, D)
```
